# Optimizing a Trainium2 kernel written in Bass

```python
import numpy as np
import jax
import jax.numpy as jnp

def _softmax(x, axis=-1):
    return jax.nn.softmax(x, axis=axis)

def _gelu(x):
    return jax.nn.gelu(x, approximate=True)

def _silu(x):
    return jax.nn.silu(x)

def _sigmoid(x):
    return jax.nn.sigmoid(x)

def _layernorm(x, axis=-1, eps=1e-05):
    m = jnp.mean(x, axis=axis, keepdims=True)
    v = jnp.var(x, axis=axis, keepdims=True)
    return (x - m) / jnp.sqrt(v + eps)

def _scatter_add(tgt, idx, src, axis=0):
    return tgt.at[idx].add(src)

def _segment_sum(src, seg, n):
    return jax.ops.segment_sum(src, seg, n)
kernel_name = 'mk_prb_d2_jaxref_r8_0c3c84'

def setup_inputs(seed: int=0):
    np.random.seed(seed)
    _w = jnp.asarray

    def _L0_attn_setup():
        import math
        import jax, jax.numpy as jnp
        import numpy as np
        B, C, D = (4, 256, 128)
        DQ = DV = 64
        H = 16
        key = jax.random.key(seed)
        kx, kq, kk, kv, kw = jax.random.split(key, 5)
        x = jax.random.normal(kx, (B, C, D), dtype=jnp.float32)
        Q = jax.random.normal(kq, (DQ, D, H), dtype=jnp.float32) / math.sqrt(D)
        K = jax.random.normal(kk, (DQ, D, H), dtype=jnp.float32) / math.sqrt(D)
        V = jax.random.normal(kv, (DV, D, H), dtype=jnp.float32) / math.sqrt(D)
        W = jax.random.normal(kw, (D, DV, H), dtype=jnp.float32) / math.sqrt(DV)
        return {'x': x, 'Q': Q, 'K': K, 'V': V, 'W': W}
    _L0_attn_in = _L0_attn_setup()

    def _L0_ffn_setup():
        import jax, jax.numpy as jnp
        import numpy as np
        H = 128
        E = 32
        I = 64
        TOP_K = 6
        IS = 128
        NORM_MIN = 1e-12
        B, S = (2, 128)
        key = jax.random.key(seed)
        ks = jax.random.split(key, 8)
        sc = 0.02
        return {'hidden_states': jax.random.normal(ks[0], (B, S, H), jnp.float32), 'router_weight': jax.random.normal(ks[1], (E, H), jnp.float32) * sc, 'e_score_bias': jnp.zeros((E,), jnp.float32), 'gate_up_proj': jax.random.normal(ks[2], (E, 2 * I, H), jnp.float32) * sc, 'down_proj': jax.random.normal(ks[3], (E, H, I), jnp.float32) * sc, 'shared_gate_w': jax.random.normal(ks[4], (IS, H), jnp.float32) * sc, 'shared_up_w': jax.random.normal(ks[5], (IS, H), jnp.float32) * sc, 'shared_down_w': jax.random.normal(ks[6], (H, IS), jnp.float32) * sc}
    _L0_ffn_in = _L0_ffn_setup()

    def _L1_attn_setup():
        import jax, jax.numpy as jnp
        import numpy as np
        D_MODEL = 128
        N_HEADS = 4
        N_KV_HEADS = 2
        HEAD_DIM = D_MODEL // N_HEADS
        N_REP = N_HEADS // N_KV_HEADS
        EPS_RMS = 1e-06
        EPS_NORM = 1e-12

        def _rmsnorm(x, w):
            var = jnp.mean(jnp.square(x), axis=-1, keepdims=True)
            return x * jax.lax.rsqrt(var + EPS_RMS) * w

        def _l2norm(x):
            n = jnp.sqrt(jnp.sum(jnp.square(x), axis=-1, keepdims=True))
            return x / jnp.maximum(n, EPS_NORM)
        key = jax.random.key(seed)
        ks = jax.random.split(key, 8)
        B, L = (2, 512)
        s = 0.02
        return {'x': jax.random.normal(ks[0], (B, L, D_MODEL), dtype=jnp.float32), 'norm_w': jnp.ones((D_MODEL,), dtype=jnp.float32), 'Wq': jax.random.normal(ks[1], (D_MODEL, N_HEADS * HEAD_DIM), dtype=jnp.float32) * s, 'Wk': jax.random.normal(ks[2], (D_MODEL, N_KV_HEADS * HEAD_DIM), dtype=jnp.float32) * s, 'Wv': jax.random.normal(ks[3], (D_MODEL, N_KV_HEADS * HEAD_DIM), dtype=jnp.float32) * s, 'Wo': jax.random.normal(ks[4], (N_HEADS * HEAD_DIM, D_MODEL), dtype=jnp.float32) * s, 'gate': jnp.asarray(0.1, dtype=jnp.float32), 'log_temperature': jnp.asarray(np.log(10.0), dtype=jnp.float32)}
    _L1_attn_in = _L1_attn_setup()

    def _L1_ffn_setup():
        import jax, jax.numpy as jnp
        import numpy as np
        GROUP = 16
        EPS = 1e-05

        def _dequant(q, scale):
            w = q.astype(jnp.float32) / 7.5 - 1.0
            return w * jnp.repeat(scale, GROUP, axis=1)

        def _qlora_linear(x, q, scale, bias, la, lb):
            w = _dequant(q, scale)
            base = jnp.einsum('btd,od->bto', x, w) + bias
            lora = jnp.einsum('btr,or->bto', jnp.einsum('btd,rd->btr', x, la), lb)
            return base + lora

        def _layernorm(x, g, b):
            mu = jnp.mean(x, axis=-1, keepdims=True)
            var = jnp.mean(jnp.square(x - mu), axis=-1, keepdims=True)
            return (x - mu) * jax.lax.rsqrt(var + EPS) * g + b
        key = jax.random.key(seed)
        ks = jax.random.split(key, 6)
        D, R, B, T = (128, 32, 8, 512)
        x = jax.random.normal(ks[0], (B, T, D), dtype=jnp.float32)
        qweights = jax.random.randint(ks[1], (6, D, D), 0, 16, dtype=jnp.int32)
        scales = jax.random.uniform(ks[2], (6, D, D // GROUP), dtype=jnp.float32)
        biases = jax.random.normal(ks[3], (6, D), dtype=jnp.float32) * 0.02
        lora_a = jax.random.normal(ks[4], (6, R, D), dtype=jnp.float32) * 0.02
        lora_b = jax.random.normal(ks[5], (6, D, R), dtype=jnp.float32) * 0.02
        ln_gamma = jnp.ones((3, D), dtype=jnp.float32)
        ln_beta = jnp.zeros((3, D), dtype=jnp.float32)
        return {'x': x, 'qweights': qweights, 'scales': scales, 'biases': biases, 'lora_a': lora_a, 'lora_b': lora_b, 'ln_gamma': ln_gamma, 'ln_beta': ln_beta}
    _L1_ffn_in = _L1_ffn_setup()
    _d = {'L0_attn_x': _L0_attn_in['x'], 'L0_attn_Q': _L0_attn_in['Q'], 'L0_attn_K': _L0_attn_in['K'], 'L0_attn_V': _L0_attn_in['V'], 'L0_attn_W': _L0_attn_in['W'], 'L0_ffn_router_weight': _L0_ffn_in['router_weight'], 'L0_ffn_e_score_bias': _L0_ffn_in['e_score_bias'], 'L0_ffn_gate_up_proj': _L0_ffn_in['gate_up_proj'], 'L0_ffn_down_proj': _L0_ffn_in['down_proj'], 'L0_ffn_shared_gate_w': _L0_ffn_in['shared_gate_w'], 'L0_ffn_shared_up_w': _L0_ffn_in['shared_up_w'], 'L0_ffn_shared_down_w': _L0_ffn_in['shared_down_w'], 'L1_attn_norm_w': _L1_attn_in['norm_w'], 'L1_attn_Wq': _L1_attn_in['Wq'], 'L1_attn_Wk': _L1_attn_in['Wk'], 'L1_attn_Wv': _L1_attn_in['Wv'], 'L1_attn_Wo': _L1_attn_in['Wo'], 'L1_attn_gate': _L1_attn_in['gate'], 'L1_attn_log_temperature': _L1_attn_in['log_temperature'], 'L1_ffn_qweights': _L1_ffn_in['qweights'], 'L1_ffn_scales': _L1_ffn_in['scales'], 'L1_ffn_biases': _L1_ffn_in['biases'], 'L1_ffn_lora_a': _L1_ffn_in['lora_a'], 'L1_ffn_lora_b': _L1_ffn_in['lora_b'], 'L1_ffn_ln_gamma': _L1_ffn_in['ln_gamma'], 'L1_ffn_ln_beta': _L1_ffn_in['ln_beta']}
    _x0 = _d['L0_attn_x']
    _d['L0_attn_x'] = jax.random.normal(jax.random.fold_in(jax.random.key(seed), 1), (8, 512, 128), dtype=_x0.dtype)
    del _x0
    return _d

def reference(L0_attn_x, L0_attn_Q, L0_attn_K, L0_attn_V, L0_attn_W, L0_ffn_router_weight, L0_ffn_e_score_bias, L0_ffn_gate_up_proj, L0_ffn_down_proj, L0_ffn_shared_gate_w, L0_ffn_shared_up_w, L0_ffn_shared_down_w, L1_attn_norm_w, L1_attn_Wq, L1_attn_Wk, L1_attn_Wv, L1_attn_Wo, L1_attn_gate, L1_attn_log_temperature, L1_ffn_qweights, L1_ffn_scales, L1_ffn_biases, L1_ffn_lora_a, L1_ffn_lora_b, L1_ffn_ln_gamma, L1_ffn_ln_beta):

    def _L0_attn_ref(x, Q, K, V, W):
        import math
        import jax, jax.numpy as jnp
        import numpy as np
        B, C, D = (4, 256, 128)
        DQ = DV = 64
        H = 16
        d_query, d_embed, num_heads = Q.shape
        d_value = V.shape[0]
        sq = math.sqrt(d_query / d_embed)
        sv = math.sqrt(d_value / d_embed)
        q = jnp.einsum('qdh,bcd->bhcq', Q, x) * sq
        k = jnp.einsum('qdh,bcd->bhcq', K, x) * sq
        v = jnp.einsum('vdh,bcd->bhcv', V, x) * sv
        att = jnp.einsum('bhcq,bhCq->bhcC', q, k) / d_query
        T = x.shape[1]
        causal = jnp.arange(T)[:, None] >= jnp.arange(T)[None, :]
        att = jnp.where(causal, att, -jnp.inf)
        p = jax.nn.softmax(att, axis=-1)
        y = jnp.einsum('bhcC,bhCv->bhcv', p, v)
        z = jnp.einsum('dvh,bhcv->bcd', W, y) * (math.sqrt(d_embed / d_value) / num_heads)
        return z

    def _L0_ffn_ref(hidden_states, router_weight, e_score_bias, gate_up_proj, down_proj, shared_gate_w, shared_up_w, shared_down_w):
        import jax, jax.numpy as jnp
        import numpy as np
        H = 128
        E = 32
        I = 64
        TOP_K = 6
        IS = 128
        NORM_MIN = 1e-12
        B, S = (2, 128)
        b, s, h = hidden_states.shape
        x = hidden_states.reshape(-1, h)
        T = x.shape[0]
        shared_out = jax.nn.silu(x @ shared_gate_w.T) * (x @ shared_up_w.T) @ shared_down_w.T
        xf = x.astype(jnp.float32)
        router_logits = xf @ router_weight.T
        routing_weights = jax.nn.softmax(router_logits, axis=-1)
        corrected = routing_weights + e_score_bias
        _, top_idx = jax.lax.top_k(corrected, TOP_K)
        top_w = jnp.take_along_axis(routing_weights, top_idx, axis=-1)
        top_w = top_w / jnp.clip(top_w.sum(axis=-1, keepdims=True), NORM_MIN)
        top_w = top_w.astype(x.dtype)
        combine = jnp.zeros((T, E), x.dtype).at[jnp.arange(T)[:, None], top_idx].add(top_w)
        gu = jnp.einsum('th,eih->tei', x, gate_up_proj)
        gate, up = jnp.split(gu, 2, axis=-1)
        hmid = jax.nn.silu(gate) * up
        y = jnp.einsum('tei,ehi->teh', hmid, down_proj)
        out = jnp.einsum('teh,te->th', y, combine) + shared_out
        return out.reshape(b, s, h)

    def _L1_attn_ref(x, norm_w, Wq, Wk, Wv, Wo, gate, log_temperature):
        import jax, jax.numpy as jnp
        import numpy as np
        D_MODEL = 128
        N_HEADS = 4
        N_KV_HEADS = 2
        HEAD_DIM = D_MODEL // N_HEADS
        N_REP = N_HEADS // N_KV_HEADS
        EPS_RMS = 1e-06
        EPS_NORM = 1e-12

        def _rmsnorm(x, w):
            var = jnp.mean(jnp.square(x), axis=-1, keepdims=True)
            return x * jax.lax.rsqrt(var + EPS_RMS) * w

        def _l2norm(x):
            n = jnp.sqrt(jnp.sum(jnp.square(x), axis=-1, keepdims=True))
            return x / jnp.maximum(n, EPS_NORM)
        B, L, D = x.shape
        h = _rmsnorm(x, norm_w)
        q = (h @ Wq).reshape(B, L, N_HEADS, HEAD_DIM).transpose(0, 2, 1, 3)
        k = (h @ Wk).reshape(B, L, N_KV_HEADS, HEAD_DIM).transpose(0, 2, 1, 3)
        v = (h @ Wv).reshape(B, L, N_KV_HEADS, HEAD_DIM).transpose(0, 2, 1, 3)
        if N_REP > 1:
            k = jnp.repeat(k, N_REP, axis=1)
            v = jnp.repeat(v, N_REP, axis=1)
        q = _l2norm(q)
        k = _l2norm(k)
        scale = jnp.exp(log_temperature)
        attn = jnp.einsum('bhqd,bhkd->bhqk', q, k) * scale
        causal = jnp.tril(jnp.ones((L, L), dtype=bool))
        attn = jnp.where(causal, attn, -jnp.inf)
        attn = jax.nn.softmax(attn, axis=-1)
        out = jnp.einsum('bhqk,bhkd->bhqd', attn, v).transpose(0, 2, 1, 3).reshape(B, L, D)
        out = out @ Wo
        return x + gate * out

    def _L1_ffn_ref(x, qweights, scales, biases, lora_a, lora_b, ln_gamma, ln_beta):
        import jax, jax.numpy as jnp
        import numpy as np
        GROUP = 16
        EPS = 1e-05

        def _dequant(q, scale):
            w = q.astype(jnp.float32) / 7.5 - 1.0
            return w * jnp.repeat(scale, GROUP, axis=1)

        def _qlora_linear(x, q, scale, bias, la, lb):
            w = _dequant(q, scale)
            base = jnp.einsum('btd,od->bto', x, w) + bias
            lora = jnp.einsum('btr,or->bto', jnp.einsum('btd,rd->btr', x, la), lb)
            return base + lora

        def _layernorm(x, g, b):
            mu = jnp.mean(x, axis=-1, keepdims=True)
            var = jnp.mean(jnp.square(x - mu), axis=-1, keepdims=True)
            return (x - mu) * jax.lax.rsqrt(var + EPS) * g + b
        h = x
        for blk in range(3):
            i0, i1 = (2 * blk, 2 * blk + 1)
            y = _qlora_linear(h, qweights[i0], scales[i0], biases[i0], lora_a[i0], lora_b[i0])
            y = _layernorm(y, ln_gamma[blk], ln_beta[blk])
            y = jax.nn.gelu(y, approximate=False)
            y = _qlora_linear(y, qweights[i1], scales[i1], biases[i1], lora_a[i1], lora_b[i1])
            h = y + h
        return h
    x = L0_attn_x
    xn = _layernorm(x, axis=-1)
    x = x + _L0_attn_ref(xn, L0_attn_Q, L0_attn_K, L0_attn_V, L0_attn_W) + _L0_ffn_ref(xn, L0_ffn_router_weight, L0_ffn_e_score_bias, L0_ffn_gate_up_proj, L0_ffn_down_proj, L0_ffn_shared_gate_w, L0_ffn_shared_up_w, L0_ffn_shared_down_w)
    xn = _layernorm(x, axis=-1)
    x = x + _L1_attn_ref(xn, L1_attn_norm_w, L1_attn_Wq, L1_attn_Wk, L1_attn_Wv, L1_attn_Wo, L1_attn_gate, L1_attn_log_temperature) + _L1_ffn_ref(xn, L1_ffn_qweights, L1_ffn_scales, L1_ffn_biases, L1_ffn_lora_a, L1_ffn_lora_b, L1_ffn_ln_gamma, L1_ffn_ln_beta)
    return x

_drawn_inputs = setup_inputs


def setup_inputs(seed=0):
    import zlib

    import numpy as np

    out = dict(_drawn_inputs(seed))
    spreads = {'L0_ffn_e_score_bias': (0.0, 0.8),
     'L1_attn_norm_w': (1.0, 0.6),
     'L1_ffn_ln_gamma': (1.0, 0.2),
     'L1_ffn_ln_beta': (0.0, 0.1)}
    factors = {'L0_attn_Q': 8.0,
     'L0_attn_K': 8.0,
     'L0_ffn_router_weight': 8.0,
     'L0_ffn_gate_up_proj': 8.0,
     'L0_ffn_down_proj': 8.0,
     'L0_ffn_shared_gate_w': 8.0,
     'L0_ffn_shared_up_w': 8.0,
     'L0_ffn_shared_down_w': 8.0,
     'L1_attn_Wq': 8.0,
     'L1_attn_Wk': 8.0,
     'L1_attn_Wv': 8.0,
     'L1_attn_Wo': 8.0,
     'L1_ffn_biases': 5.727,
     'L1_ffn_lora_a': 5.651,
     'L1_ffn_lora_b': 5.716}
    for name, (base, spread) in spreads.items():
        noise = np.random.default_rng([zlib.crc32(name.encode()), seed]).standard_normal(out[name].shape)
        drawn = base * np.exp(spread * noise) if base else spread * noise
        out[name] = jnp.asarray(drawn.astype(out[name].dtype))
    for name, factor in factors.items():
        out[name] = (out[name] * factor).astype(out[name].dtype)
    return out
```

```python
from contextlib import ExitStack

import concourse.bass as bass
from concourse import mybir

F32 = mybir.dt.float32
F32R = mybir.dt.float32r
BF16 = mybir.dt.bfloat16
I32 = mybir.dt.int32
U32 = mybir.dt.uint32
ACT = mybir.ActivationFunctionType
ALU = mybir.AluOpType
AX = mybir.AxisListType.X

P = 128
B, T, D = 8, 512, 128
TILES = T // P
H0, DQ = 16, 64
PAIRS = H0 // 2
E, I, TOPK = 32, 64, 6
UNITS = 1 + E // 2
H1, KV1, HD1 = 4, 2, 32
QKV1 = (H1 + 2 * KV1) * HD1
R, GROUP, NLIN = 32, 16, 6
BLOCKS = NLIN // 2
EPS = 1e-5
EPS_RMS = 1e-6
EPS_L2 = 1e-12
NORM_MIN = 1e-12
NEG = -1e30
SCALE0 = (DQ / D) / DQ
OUT0 = 1.0 / H0
ROUNDS = PAIRS + H1 // 2
QKS = PAIRS + 1

SOFF = [[0, 512, 1024, 896], [1536, 2048, 1280, 2432]]
HALF = 5 * 512 // 2
DIAG = [[(0, 512, 2), (896, 128, 2)], [(1536, 512, 2), (1280, 0, 1), (2432, 0, 1)]]
CHUNKS = [[(h, 3, 0)] if c == 0 else [(h, 2, 0), (h, 0, 384)] if c == 1 else [(h, 1, 0)] for h in range(2) for c in range(3)]
NCH = len(CHUNKS)


def split_matmul(nc, out, lhs, rhs, start, stop, **kw):
    (lh, ll), (rh, rl) = lhs, rhs
    nc.tensor.matmul(out, lh, rh, start=start, stop=False, **kw)
    nc.tensor.matmul(out, lh, rl, start=False, stop=False, **kw)
    return nc.tensor.matmul(out, ll, rh, start=False, stop=stop, **kw)


class Chain:

    def __init__(self, eng, sem, base):
        self.eng, self.sem, self.base, self.n = eng, sem, base, 0

    def step(self, ins):
        ins.then_inc(self.sem, 1)
        self.n += 1
        self.eng.wait_ge(self.sem, self.base + self.n)
        return self


def build(nc, a, out_dram):
    with ExitStack() as ctx:
        def sb(name, shape, dt=F32):
            return ctx.enter_context(nc.sbuf_tensor(name, shape, dt))

        def sem(name):
            return ctx.enter_context(nc.semaphore(name))

        x_all = sb("x_all", [P, B, TILES, D])
        wraw = sb("wraw", [P, UNITS, 2 * P])
        wqkv_raw = wraw[:, 0:12, :].rearrange("p u n -> p (u n)")
        wqkv_hi = sb("wqkv_hi", [P, 3, PAIRS, P], F32R)
        wqkv_lo = sb("wqkv_lo", [P, 3, PAIRS, P], F32R)
        gu_hi = sb("gu_hi", [P, UNITS, 2 * P], F32R)
        gu_lo = sb("gu_lo", [P, UNITS, 2 * P], F32R)
        down = sb("down", [P, UNITS, D])
        w_out0 = sb("w_out0", [P, PAIRS, D])
        rw_raw = sb("rw_raw", [P, E])
        rw_hi = sb("rw_hi", [P, E], F32R)
        rw_lo = sb("rw_lo", [P, E], F32R)
        ebias = sb("ebias", [P, E])
        wqkv1 = sb("wqkv1", [P, QKV1])
        norm_w = sb("norm_w", [P, 1])
        wo1 = sb("wo1", [P, D])
        gate1 = sb("gate1", [P, 1])
        temp1 = sb("temp1", [P, 2])
        qw = sb("qw", [P, NLIN, D], I32)
        qs = sb("qs", [P, NLIN, D])
        lin = sb("lin", [P, NLIN, D])
        la = sb("la", [R, NLIN, D])
        lb = sb("lb", [R, NLIN, D])
        bias_col = sb("bias_col", [P, NLIN])
        bias_row = sb("bias_row", [1, NLIN, D])
        ln_g = sb("ln_g", [P, BLOCKS])
        ln_b = sb("ln_b", [P, BLOCKS])

        ident = sb("ident", [P, P])
        identb = sb("identb", [P, P], BF16)
        causal = sb("causal", [P, P], BF16)
        msel = sb("msel", [P, 2, P], BF16)
        csel = sb("csel", [P, UNITS, P], BF16)
        ones = sb("ones", [P, P])
        mhalf = sb("mhalf", [P, 32])
        iota_e = sb("iota_e", [P, E])
        iota_i = sb("iota_i", [P, E], I32)

        stats = sb("stats", [P, TILES, 6])
        mv = sb("mv", [P, TILES, 2])
        var = sb("var", [P, TILES])
        rstd = sb("rstd", [P, TILES])
        xn = sb("xn", [P, TILES, D])
        xt_hi = sb("xt_hi", [P, T], F32R)
        xt_lo = sb("xt_lo", [P, T], F32R)
        wst_hi = sb("wst_hi", [P, 2, P], F32R)
        wst_lo = sb("wst_lo", [P, 2, P], F32R)
        qk_hi = sb("qk_hi", [P, 2, T], F32R)
        qk_lo = sb("qk_lo", [P, 2, T], F32R)
        v0 = sb("v0", [P, TILES, P])
        mneg = sb("mneg", [P, TILES, 2])
        msplit = sb("msplit", [P, TILES, 4], BF16)
        mrow = sb("mrow", [P, T], BF16)
        probs = [sb(f"probs{i}", [P, 5 * 512]) for i in range(2)]
        psums = [sb(f"psums{i}", [P, 2, T]) for i in range(2)]
        rinv = sb("rinv", [P, T])
        yt = sb("yt", [P, PAIRS, T])

        rl = sb("rl", [P, TILES, E])
        rsmall = sb("rsmall", [P, 4, TILES])
        corr = sb("corr", [P, TILES, E])
        top8 = sb("top8", [P, TILES, 8])
        idx8 = sb("idx8", [P, TILES, 8], U32)
        idxf = sb("idxf", [P, TILES, 8])
        onehot = psums[1][:, :, :].rearrange("p h t -> p (h t)")[:, 0:TILES * E * TOPK].rearrange("p (t e k) -> p t e k", t=TILES, e=E)
        comb = sb("comb", [P, TILES, E])
        comb3 = sb("comb3", [P, TILES, P], BF16)
        combt = sb("combt", [P, T], BF16)
        gst_hi = sb("gst_hi", [P, 2, 2 * P], F32R)
        gst_lo = sb("gst_lo", [P, 2, 2 * P], F32R)
        sg = probs[1][:, 0 * 2 * T:1 * 2 * T].rearrange("p (s t) -> p s t", s=2)
        hm = probs[1][:, 1 * 2 * T:2 * 2 * T].rearrange("p (s t) -> p s t", s=2)

        junk = sb("junk", [P, D])
        ss1 = sb("ss1", [P, TILES, H1 + KV1])
        rn1 = sb("rn1", [P, TILES, H1 + KV1])
        layer1 = yt[:, :, :].rearrange("p n t -> p (n t)")
        x1, xr, zn = (layer1[:, n * T:(n + 1) * T].rearrange("p (t d) -> p t d", t=TILES) for n in range(3))
        ht, gt, y1t = (layer1[:, n * T:(n + 1) * T] for n in range(3, 6))
        qkv1 = layer1[:, 6 * T:8 * T].rearrange("p (t n) -> p t n", t=TILES)
        sq1 = probs[0][:, 0:TILES * (H1 + KV1) * HD1].rearrange("p (t n) -> p t n", t=TILES)
        qn1, kn1 = (probs[0][:, n * T:(n + 1) * T].rearrange("p (t n) -> p t n", t=TILES) for n in (2, 3))

        psum = ctx.enter_context(nc.psum_tensor("psum", [P, 8, 512], F32))
        scores = psum[:, 0:5, :].rearrange("p b n -> p (b n)")
        bank = [psum[:, i, :] for i in range(8)]
        R0, R1, R2 = bank[5], bank[6], bank[7]
        CHUNK_BANK = [R2, R0, R2, R0, R0, R0]
        PREV = {2: 0, 3: 1, 4: 3, 5: 4}

        x_loaded = sem("x_loaded")
        qkvw_loaded = sem("qkvw_loaded")
        guw_loaded = sem("guw_loaded")
        w_loaded = sem("w_loaded")
        const_ready = sem("const_ready")
        pool_setup = sem("pool_setup")
        hi_setup = sem("hi_setup")
        lo_setup = sem("lo_setup")
        dve_setup = sem("dve_setup")
        act_setup = sem("act_setup")
        lora_done = sem("lora_done")
        dve_chain = sem("dve_chain")
        pool_chain = sem("pool_chain")
        act_chain = sem("act_chain")
        var_ready = sem("var_ready")
        rstd_ready = sem("rstd_ready")
        row_ready = sem("row_ready")
        tr_done = sem("tr_done")
        xt_hi_ready = sem("xt_hi_ready")
        xt_lo_ready = sem("xt_lo_ready")
        logits_done = sem("logits_done")
        rl_ready = sem("rl_ready")
        rexp_done = sem("rexp_done")
        comb_ready = sem("comb_ready")
        combt_done = sem("combt_done")
        combt_ready = sem("combt_ready")
        wst_ready = sem("wst_ready")
        qk_done = sem("qk_done")
        qk_split = sem("qk_split")
        v_done = sem("v_done")
        v_ready = sem("v_ready")
        max_done = sem("max_done")
        max_read = sem("max_read")
        m_ready = sem("m_ready")
        mrow_done = sem("mrow_done")
        mrow_ready = sem("mrow_ready")
        scores_done = sem("scores_done")
        exp_done = sem("exp_done")
        masked = sem("masked")
        presum_step = sem("presum_step")
        s_done = sem("s_done")
        s_read = sem("s_read")
        y_ready = sem("y_ready")
        gst_ready = sem("gst_ready")
        gu_done = sem("gu_done")
        silu_done = sem("silu_done")
        su_done = sem("su_done")
        hm_ready = sem("hm_ready")
        down_done = sem("down_done")
        x1_ready = sem("x1_ready")
        sumsq_ready = sem("sumsq_ready")
        rms_ready = sem("rms_ready")
        xr_ready = sem("xr_ready")
        ht_ready = sem("ht_ready")
        qkv1_done = sem("qkv1_done")
        qkv1_ready = sem("qkv1_ready")
        sq1_ready = sem("sq1_ready")
        ss1_ready = sem("ss1_ready")
        rn1_ready = sem("rn1_ready")
        qkn_ready = sem("qkn_ready")
        qkt_done = sem("qkt_done")
        y1_done = sem("y1_done")
        y1t_ready = sem("y1t_ready")
        lin_done = sem("lin_done")
        zn_ready = sem("zn_ready")
        znt_done = sem("znt_done")
        gt_ready = sem("gt_ready")
        f_done = sem("f_done")
        h_ready = sem("h_ready")
        x2_done = sem("x2_done")
        x2_ready = sem("x2_ready")
        stored = sem("stored")
        shared_bank = sem("shared_bank")
        waits_over = sem("waits_over")

        block = ctx.enter_context(nc.Block())

        def wait_alone(eng, s, value):
            eng.wait_ge(s, value)
            eng.sem_inc(waits_over, 1)

        x_v = a["x"].rearrange("b (t p) d -> b p t d", p=P)
        out_v = out_dram.rearrange("b (t p) d -> b p t d", p=P)

        @block.sync
        def _(sp):
            sp.dma_start(x_all[:, 0, :, :], x_v[0, :, :, :]).then_inc(x_loaded, 16)
            sp.dma_start(wqkv_raw, a["wqkv"]).then_inc(qkvw_loaded, 16)
            for i in range(1, B):
                sp.dma_start(x_all[:, i, :, :], x_v[i, :, :, :]).then_inc(x_loaded, 16)
            sp.wait_ge(lo_setup, 1)
            sp.dma_start(wraw[:, :, :], a["gu"]).then_inc(guw_loaded, 16)
            with sp.Fori(0, B) as b:
                dst = out_v[b, :, :, :]
                src = x_all[:, b, :, :]
                sp.wait_ge(x2_ready, b + 1)
                sp.dma_start(dst, src).then_inc(stored, 16)
            sp.wait_ge(stored, 16 * B)

        small_loads = [
            (rw_raw[:, :], a["router"]), (ebias[:, :], a["ebias"].partition_broadcast(P)),
            (w_out0[:, :, :], a["w_out0"]), (down[:, :, :], a["down"]),
            (wqkv1[:, :], a["wqkv1"]), (norm_w[:, :], a["norm_w"]), (wo1[:, :], a["wo1"]),
            (gate1[:, :], a["gate1"].partition_broadcast(P)), (temp1[:, 0:1], a["temp1"].partition_broadcast(P)),
            (qw[:, :, :], a["qw"]), (la[:, :, :], a["la"]), (lb[:, :, :], a["lb"]),
            (bias_col[:, :], a["bias_col"]), (ln_g[:, :], a["ln_g"]), (ln_b[:, :], a["ln_b"]),
        ]
        small_loads += [(bias_row[:, :, :], a["bias_row"])]
        small_loads += [(qs[g * GROUP:(g + 1) * GROUP, :, :], a["qs"][g, :, :].partition_broadcast(GROUP)) for g in range(D // GROUP)]
        W_LOADS = 16 * len(small_loads)

        @block.gpsimd
        def _(pool):
            setup = Chain(pool, pool_setup, 0)
            pool.memset(ident[:, :], 0.0).then_inc(pool_setup, 1)
            pool.memset(identb[:, :], 0.0).then_inc(pool_setup, 1)
            pool.memset(causal[:, :], 0.0).then_inc(pool_setup, 1)
            pool.memset(msel[:, :, :], 0.0).then_inc(pool_setup, 1)
            pool.memset(csel[:, :, :], 0.0).then_inc(pool_setup, 1)
            pool.memset(mrow[:, :], 0.0).then_inc(pool_setup, 1)
            pool.memset(mhalf[:, :], -0.5).then_inc(pool_setup, 1)
            pool.memset(ones[:, :], 1.0).then_inc(pool_setup, 1)
            setup.n = 8
            setup.step(pool.memset(comb3[:, :, :], 0.0))
            pool.memset(comb3[:, :, 3 * E:3 * E + 1], 1.0).then_inc(pool_setup, 1)
            setup.n += 1
            for m in (ident, identb):
                setup.step(pool.affine_select(out=m[:, :], in_=m[:, :], compare_op=ALU.not_equal, fill=1.0, base=0,
                                              pattern=[[-1, P]], channel_multiplier=1))
            setup.step(pool.affine_select(out=causal[:, :], in_=causal[:, :], compare_op=ALU.is_ge, fill=NEG, base=0,
                                          pattern=[[-1, P]], channel_multiplier=1))
            for part in range(2):
                setup.step(pool.affine_select(out=msel[:, :, :], in_=msel[:, :, :], compare_op=ALU.not_equal, fill=1.0,
                                              base=-2 * part, pattern=[[-1, 2], [0, P]], channel_multiplier=1))
            pairs_v = csel[:, 1:UNITS, :].rearrange("p u (h m) -> p u h m", h=2)
            for part in range(3):
                setup.step(pool.affine_select(out=pairs_v, in_=pairs_v, compare_op=ALU.not_equal, fill=1.0,
                                              base=-E * part, pattern=[[-2, UNITS - 1], [-1, 2], [0, I]], channel_multiplier=1))
            setup.step(pool.affine_select(out=csel[:, 0, :], in_=csel[:, 0, :], compare_op=ALU.not_equal, fill=1.0,
                                          base=-3 * E, pattern=[[0, P]], channel_multiplier=1))
            setup.step(pool.iota(iota_i[:, :], pattern=[[1, E]], base=0, channel_multiplier=0))
            pool.tensor_copy(iota_e[:, :], iota_i[:, :]).then_inc(const_ready, 1)
            pool.wait_ge(const_ready, 1)

            def stage_qk(n, p):
                pool.tensor_copy(wst_hi[:, :, :], wqkv_hi[:, 0:2, p, :]).then_inc(wst_ready, 1)
                pool.tensor_copy(wst_lo[:, :, :], wqkv_lo[:, 0:2, p, :]).then_inc(wst_ready, 1)

            def mask_and_presum(rnd, j):
                for h in range(2):
                    wait_alone(pool, exp_done, 2 * rnd + h + 1)
                    for first, stride, n in DIAG[h]:
                        v = probs[j][:, first:first + max(stride, P) * n].rearrange("p (n q) -> p n q", n=n)[:, :, 0:P]
                        pool.affine_select(out=v, in_=v, compare_op=ALU.is_ge, fill=0.0, base=0,
                                           pattern=[[0, n], [1, P]], channel_multiplier=-1).then_inc(masked, 1)
                for h in range(2):
                    pool.wait_ge(masked, 5 * rnd + (2, 5)[h])
                    o = SOFF[h]
                    acc = psums[j][:, h, :]
                    n = 6 * rnd + 3 * h
                    pool.tensor_tensor(acc[:, P:T], probs[j][:, o[0] + P:o[0] + T], probs[j][:, o[1]:o[1] + 3 * P],
                                       ALU.add).then_inc(presum_step, 1)
                    pool.wait_ge(presum_step, n + 1)
                    pool.tensor_tensor(acc[:, 2 * P:T], acc[:, 2 * P:T], probs[j][:, o[2]:o[2] + 2 * P],
                                       ALU.add).then_inc(presum_step, 1)
                    pool.wait_ge(presum_step, n + 2)
                    pool.tensor_tensor(acc[:, 3 * P:T], acc[:, 3 * P:T], probs[j][:, o[3]:o[3] + P],
                                       ALU.add).then_inc(presum_step, 1)

            def stage_gu(n, u, s):
                pool.tensor_copy(gst_hi[:, s, :], gu_hi[:, u, :]).then_inc(gst_ready, 1)
                pool.tensor_copy(gst_lo[:, s, :], gu_lo[:, u, :]).then_inc(gst_ready, 1)

            with pool.Fori(0, B) as b:
                chain = Chain(pool, pool_chain, 0)

                def inv_sqrt(n):
                    pool.wait_ge(var_ready, b * 5 + n + 1)
                    pool.tensor_tensor(rstd[:, :], var[:, :], mhalf[:, 0:TILES], ALU.pow).then_inc(rstd_ready, 1)

                inv_sqrt(0)
                pool.wait_ge(lo_setup, 1)
                pool.wait_ge(hi_setup, 1)
                stage_qk(b * PAIRS, 0)
                wait_alone(pool, qk_done, b * PAIRS + 1)
                stage_qk(b * PAIRS + 1, 1)
                with pool.Fori(0, PAIRS - 2) as p:
                    mask_and_presum(b * ROUNDS + p, 0)
                    wait_alone(pool, qk_done, b * PAIRS + p + 2)
                    stage_qk(b * PAIRS + p + 2, p + 2)
                for p in (PAIRS - 2, PAIRS - 1):
                    mask_and_presum(b * ROUNDS + p, 0)
                pool.wait_ge(lo_setup, 2)
                for u in range(3):
                    if u == 2:
                        wait_alone(pool, gu_done, b * UNITS + 1)
                    stage_gu(b * UNITS + u, u, u % 2)
                with pool.Fori(0, (UNITS - 3) // 2) as i:
                    for s in range(2):
                        wait_alone(pool, gu_done, b * UNITS + i * 2 + s + 2)
                        stage_gu(b * UNITS + i * 2 + s + 3, i * 2 + (s + 3), (s + 1) % 2)
                inv_sqrt(1)
                pool.wait_ge(sumsq_ready, b + 1)
                pool.tensor_tensor(rsmall[:, 0, :], rsmall[:, 1, :], mhalf[:, 0:TILES], ALU.pow).then_inc(rms_ready, 1)
                for k in range(BLOCKS):
                    inv_sqrt(2 + k)
                pool.wait_ge(ss1_ready, b + 1)
                pool.tensor_tensor(rn1[:, :, :].rearrange("p t h -> p (t h)"), ss1[:, :, :].rearrange("p t h -> p (t h)"),
                                   mhalf[:, 0:TILES * (H1 + KV1)], ALU.pow).then_inc(rn1_ready, 1)
                for j in range(2):
                    mask_and_presum(b * ROUNDS + PAIRS + j, j)

        @block.scalar
        def _(act):
            for dst, src in small_loads:
                act.dma_start(dst, src).then_inc(w_loaded, 16)
            act.wait_ge(qkvw_loaded, 16)
            act.activation(wqkv_hi[:, :, :, :].rearrange("p a b n -> p (a b n)"), wqkv_raw, ACT.Copy).then_inc(hi_setup, 1)
            act.wait_ge(w_loaded, W_LOADS)
            act.activation(rw_hi[:, :], rw_raw[:, :], ACT.Copy).then_inc(act_setup, 1)
            act.activation(w_out0[:, :, :], w_out0[:, :, :], ACT.Copy, scale=OUT0).then_inc(act_setup, 1)
            act.activation(wqkv1[:, :], wqkv1[:, :], ACT.Copy, scale=norm_w[:, 0:1]).then_inc(act_setup, 1)
            act.activation(wo1[:, :], wo1[:, :], ACT.Copy, scale=gate1[:, 0:1]).then_inc(act_setup, 1)
            act.activation(temp1[:, 1:2], temp1[:, 0:1], ACT.Exp).then_inc(act_setup, 1)
            act.wait_ge(guw_loaded, 16)
            act.activation(gu_hi[:, :, :], wraw[:, :, :], ACT.Copy).then_inc(hi_setup, 1)

            def exps(rnd, j, scale):
                for h in range(2):
                    act.wait_ge(scores_done, 2 * rnd + h + 1)
                    act.activation(probs[j][:, h * HALF:(h + 1) * HALF], scores[:, h * HALF:(h + 1) * HALF], ACT.Exp,
                                   scale=scale).then_inc(exp_done, 1)

            def copy_v(n):
                act.wait_ge(v_done, n + 1)
                act.activation(v0[:, :, :].rearrange("p t n -> p (t n)"), R2, ACT.Copy).then_inc(v_ready, 1)

            def silu(n, s, wait_buffer):
                act.wait_ge(gu_done, n + 1)
                if wait_buffer:
                    act.wait_ge(hm_ready, n - 1)
                act.activation(sg[:, s, :], bank[3 * s], ACT.Silu).then_inc(silu_done, 1)

            with act.Fori(0, B) as b:
                act.wait_ge(tr_done, b * 2 + 1)
                act.activation(xt_hi[:, :], R0, ACT.Copy).then_inc(xt_hi_ready, 1)
                act.wait_ge(rl_ready, b + 1)
                act.activation(corr[:, :, :], rl[:, :, :], ACT.Exp).then_inc(rexp_done, 1)
                copy_v(b * PAIRS)
                with act.Fori(0, PAIRS - 1) as p:
                    exps(b * ROUNDS + p, 0, SCALE0)
                    copy_v(b * PAIRS + p + 1)
                exps(b * ROUNDS + PAIRS - 1, 0, SCALE0)
                for u in range(3):
                    silu(b * UNITS + u, u % 2, u == 2)
                with act.Fori(0, (UNITS - 3) // 2) as i:
                    for s in range(2):
                        silu(b * UNITS + i * 2 + (s + 3), (s + 1) % 2, True)
                act.wait_ge(down_done, b * (UNITS + 1) + UNITS + 1)
                act.activation(x1.rearrange("p t d -> p (t d)"), R2, ACT.Copy).then_inc(x1_ready, 1)
                act.wait_ge(row_ready, b * 2 + 2)
                for t in range(TILES):
                    ins = act.activation(junk[:, :], xn[:, t, :], ACT.Square, accum_out=rsmall[:, 2, t:t + 1])
                    ins.then_inc(act_chain, 1)
                    act.wait_ge(act_chain, b * TILES + t + 1)
                act.wait_ge(tr_done, b * 2 + 2)
                act.activation(ht, R0, ACT.Copy).then_inc(ht_ready, 1)
                act.wait_ge(qkv1_done, b + 1)
                act.activation(qkv1.rearrange("p t n -> p (t n)"), psum[:, 0:2, :].rearrange("p b n -> p (b n)"),
                               ACT.Copy).then_inc(qkv1_ready, 1)
                for k in range(BLOCKS):
                    act.wait_ge(znt_done, b * BLOCKS + k + 1)
                    act.activation(gt, R1, ACT.Gelu, scale=ln_g[:, k:k + 1], bias=ln_b[:, k:k + 1]).then_inc(gt_ready, 1)
                for j in range(2):
                    exps(b * ROUNDS + PAIRS + j, j, temp1[:, 1:2])
                act.wait_ge(x2_done, b + 1)
                act.activation(x_all[:, b, :, :].rearrange("p t d -> p (t d)"), bank[0], ACT.Copy).then_inc(x2_ready, 1)

        DVE_LINKS = 31

        @block.vector
        def _(dve):
            dve.wait_ge(hi_setup, 1)
            dve.tensor_tensor(wqkv_lo[:, :, :, :].rearrange("p a b n -> p (a b n)"), wqkv_raw,
                              wqkv_hi[:, :, :, :].rearrange("p a b n -> p (a b n)").bitcast(F32), ALU.subtract).then_inc(lo_setup, 1)
            dve.wait_ge(w_loaded, W_LOADS)
            dve.wait_ge(act_setup, 1)
            dve.tensor_tensor(rw_lo[:, :], rw_raw[:, :], rw_hi[:, :].bitcast(F32), ALU.subtract).then_inc(dve_setup, 1)
            dve.tensor_copy(lin[:, :, :], qw[:, :, :]).then_inc(dve_setup, 1)
            dve.wait_ge(dve_setup, 2)
            dve.tensor_scalar(lin[:, :, :], lin[:, :, :], 1.0 / 7.5, -1.0, ALU.mult, ALU.add).then_inc(dve_setup, 1)
            dve.wait_ge(dve_setup, 3)
            dve.tensor_tensor(lin[:, :, :], lin[:, :, :], qs[:, :, :], ALU.mult).then_inc(dve_setup, 1)
            dve.wait_ge(dve_setup, 4)
            dve.wait_ge(lora_done, 1)
            lin_v = lin[:, :, :].rearrange("p i o -> p (i o)")
            dve.tensor_tensor(lin_v[:, 0:512], lin_v[:, 0:512], bank[0], ALU.add).then_inc(dve_setup, 1)
            dve.tensor_tensor(lin_v[:, 512:768], lin_v[:, 512:768], bank[1][:, 0:256], ALU.add).then_inc(dve_setup, 1)
            dve.wait_ge(hi_setup, 2)
            dve.tensor_tensor(gu_lo[:, :, :], wraw[:, :, :], gu_hi[:, :, :].bitcast(F32), ALU.subtract).then_inc(lo_setup, 1)
            dve.wait_ge(const_ready, 1)

            def split_qk(n):
                v = psum[:, 5:7, :]
                dve.tensor_copy(qk_hi[:, :, :], v).then_inc(qk_split, 1)
                dve.wait_ge(qk_split, 2 * n + 1)
                dve.tensor_tensor(qk_lo[:, :, :], v, qk_hi[:, :, :].bitcast(F32), ALU.subtract).then_inc(qk_split, 1)

            def reduce_chunk(rnd, c):
                dve.wait_ge(max_done, rnd * NCH + c + 1)
                rb = CHUNK_BANK[c]
                for h, t, o in CHUNKS[c]:
                    last = dve.tensor_reduce(mneg[:, t, h:h + 1], rb[:, o:o + P * (t + 1)], AX, ALU.max, negate=True)
                last.then_inc(max_read, 1)

            def split_m(rnd):
                dve.wait_ge(max_read, rnd * NCH + NCH)
                dve.tensor_copy(msplit[:, :, 0:2], mneg[:, :, :]).then_inc(m_ready, 1)
                dve.wait_ge(m_ready, 2 * rnd + 1)
                dve.tensor_tensor(msplit[:, :, 2:4], mneg[:, :, :], msplit[:, :, 0:2], ALU.subtract).then_inc(m_ready, 1)

            def copy_mrow(rnd):
                dve.wait_ge(mrow_done, rnd + 1)
                dve.tensor_copy(mrow[0:4, :], R1.bitcast(BF16)[0:4, 0:T]).then_inc(mrow_ready, 1)

            def normalise(n, dst):
                dve.wait_ge(s_done, n + 1)
                dve.reciprocal(rinv[:, :], R2).then_inc(s_read, 1)
                dve.wait_ge(s_read, n + 1)
                dve.tensor_tensor(dst, R1, rinv[:, :], ALU.mult).then_inc(y_ready, 1)

            def hidden(n, s, wait_buffer):
                dve.wait_ge(silu_done, n + 1)
                dve.tensor_tensor(sg[:, s, :], sg[:, s, :], bank[3 * s + 1], ALU.mult).then_inc(su_done, 1)
                dve.wait_ge(su_done, n + 1)
                if wait_buffer is not None:
                    dve.wait_ge(down_done, wait_buffer)
                dve.tensor_tensor(hm[:, s, :], sg[:, s, :], bank[3 * s + 2], ALU.mult).then_inc(hm_ready, 1)

            with dve.Fori(0, B) as b:
                chain = Chain(dve, dve_chain, b * DVE_LINKS)

                def layer_norm(n, src, dst, out_sem):
                    for t in range(TILES):
                        last = dve.bn_stats(stats[:, t, :], src[:, t, :])
                    chain.step(last)
                    dve.sem_inc(waits_over, 1)
                    for t in range(TILES):
                        last = dve.bn_aggr(mv[:, t, :], stats[:, t, :])
                    chain.step(last)
                    dve.tensor_scalar(var[:, :], mv[:, :, 1], EPS, None, ALU.add).then_inc(var_ready, 1)
                    dve.wait_ge(rstd_ready, b * 5 + n + 1)
                    for t in range(TILES):
                        last = dve.tensor_scalar(dst[:, t, :], src[:, t, :], mv[:, t, 0:1], rstd[:, t:t + 1],
                                                 ALU.subtract, ALU.mult)
                    last.then_inc(out_sem, 1)

                dve.wait_ge(x_loaded, 16 * B)
                layer_norm(0, x_all[:, b, :, :], xn, row_ready)
                dve.wait_ge(xt_hi_ready, b + 1)
                dve.tensor_tensor(xt_lo[:, :], R0, xt_hi[:, :].bitcast(F32), ALU.subtract).then_inc(xt_lo_ready, 1)
                dve.wait_ge(logits_done, b + 1)
                lg = R1[:, 0:TILES * E].rearrange("p (t e) -> p t e", e=E)
                mx, sm, ri = rsmall[:, 0, :], rsmall[:, 1, :], rsmall[:, 2, :]
                chain.step(dve.tensor_reduce(mx, lg, AX, ALU.max, negate=True))
                dve.tensor_tensor(rl[:, :, :], lg, mx.unsqueeze(2).to_broadcast([P, TILES, E]), ALU.add).then_inc(rl_ready, 1)
                dve.wait_ge(rexp_done, b + 1)
                chain.step(dve.tensor_reduce(sm, corr[:, :, :], AX, ALU.add))
                chain.step(dve.reciprocal(ri, sm))
                chain.step(dve.tensor_tensor(rl[:, :, :], corr[:, :, :], ri.unsqueeze(2).to_broadcast([P, TILES, E]), ALU.mult))
                chain.step(dve.tensor_tensor(corr[:, :, :], rl[:, :, :], ebias[:, :].unsqueeze(1).to_broadcast([P, TILES, E]), ALU.add))
                dve.sem_inc(waits_over, 1)
                for t in range(TILES):
                    last = dve.max(top8[:, t, :], corr[:, t, :])
                chain.step(last)
                dve.sem_inc(waits_over, 1)
                for t in range(TILES):
                    last = dve.max_index(idx8[:, t, :], top8[:, t, :], corr[:, t, :])
                chain.step(last)
                chain.step(dve.tensor_copy(idxf[:, :, :], idx8[:, :, :]))
                for t in range(TILES):
                    last = dve.tensor_tensor(onehot[:, t, :, :], iota_e[:, :].unsqueeze(2).to_broadcast([P, E, TOPK]),
                                             idxf[:, t, 0:TOPK].unsqueeze(1).to_broadcast([P, E, TOPK]), ALU.is_equal)
                chain.step(last)
                chain.step(dve.tensor_reduce(comb[:, :, :], onehot, AX, ALU.add))
                chain.step(dve.tensor_tensor(comb[:, :, :], comb[:, :, :], rl[:, :, :], ALU.mult))
                chain.step(dve.tensor_reduce(sm, comb[:, :, :], AX, ALU.add))
                chain.step(dve.tensor_scalar(sm, sm, NORM_MIN, None, ALU.max))
                chain.step(dve.reciprocal(ri, sm))
                chain.step(dve.tensor_tensor(comb[:, :, :], comb[:, :, :], ri.unsqueeze(2).to_broadcast([P, TILES, E]), ALU.mult))
                chain.step(dve.tensor_copy(comb3[:, :, 0:E], comb[:, :, :]))
                chain.step(dve.tensor_tensor(comb[:, :, :], comb[:, :, :], comb3[:, :, 0:E], ALU.subtract))
                chain.step(dve.tensor_copy(comb3[:, :, E:2 * E], comb[:, :, :]))
                dve.tensor_tensor(comb3[:, :, 2 * E:3 * E], comb[:, :, :], comb3[:, :, E:2 * E], ALU.subtract).then_inc(comb_ready, 1)
                dve.wait_ge(combt_done, b + 1)
                dve.tensor_copy(combt[:, :], bank[0].bitcast(BF16)[:, 0:T]).then_inc(combt_ready, 1)

                dve.wait_ge(qk_done, b * PAIRS + 1)
                split_qk(b * QKS)
                for c in range(NCH):
                    reduce_chunk(b * ROUNDS, c)
                split_m(b * ROUNDS)
                with dve.Fori(0, PAIRS - 1) as p:
                    rnd = b * ROUNDS + p
                    copy_mrow(rnd)
                    dve.wait_ge(qk_done, b * PAIRS + p + 2)
                    split_qk(b * QKS + p + 1)
                    for c in range(4):
                        reduce_chunk(rnd + 1, c)
                    normalise(b * (PAIRS + 1) + p, yt[:, p, :])
                    for c in range(4, NCH):
                        reduce_chunk(rnd + 1, c)
                    split_m(rnd + 1)
                copy_mrow(b * ROUNDS + PAIRS - 1)
                normalise(b * (PAIRS + 1) + PAIRS - 1, yt[:, PAIRS - 1, :])

                for u in range(3):
                    hidden(b * UNITS + u, u % 2, b * (UNITS + 1) + 2 if u == 2 else None)
                with dve.Fori(0, (UNITS - 3) // 2) as i:
                    for s in range(2):
                        hidden(b * UNITS + i * 2 + (s + 3), (s + 1) % 2, b * (UNITS + 1) + i * 2 + (s + 3))

                dve.wait_ge(x1_ready, b + 1)
                layer_norm(1, x1, xn, row_ready)
                dve.wait_ge(row_ready, b * 2 + 2)
                dve.tensor_tensor(xr, x1, xn[:, :, :], ALU.add).then_inc(xr_ready, 1)
                dve.wait_ge(act_chain, b * TILES + TILES)
                dve.tensor_scalar(rsmall[:, 1, :], rsmall[:, 2, :], 1.0 / D, EPS_RMS, ALU.mult, ALU.add).then_inc(sumsq_ready, 1)
                for k in range(BLOCKS):
                    dve.wait_ge(lin_done, b * BLOCKS + k + 1)
                    layer_norm(2 + k, R0.rearrange("p (t d) -> p t d", t=TILES), zn, zn_ready)
                    if k < BLOCKS - 1:
                        dve.wait_ge(f_done, b * (BLOCKS - 1) + k + 1)
                        dve.scalar_tensor_tensor(ht, R2, bias_col[:, 2 * k + 1:2 * k + 2], ht,
                                                 ALU.add, ALU.add).then_inc(h_ready, 1)
                dve.wait_ge(rms_ready, b + 1)
                dve.wait_ge(qkv1_ready, b + 1)
                chain.step(dve.tensor_tensor(qkv1, qkv1,
                                             rsmall[:, 0, :].unsqueeze(2).to_broadcast([P, TILES, QKV1]), ALU.mult))
                QK = (H1 + KV1) * HD1
                chain.step(dve.tensor_tensor(sq1, qkv1[:, :, 0:QK], qkv1[:, :, 0:QK], ALU.mult))
                chain.step(dve.tensor_reduce(ss1[:, :, :], sq1.rearrange("p t (h d) -> p t h d", d=HD1), AX, ALU.add))
                dve.tensor_scalar(ss1[:, :, :], ss1[:, :, :], EPS_L2 * EPS_L2, None, ALU.max).then_inc(ss1_ready, 1)
                dve.wait_ge(rn1_ready, b + 1)
                qv = qkv1[:, :, 0:H1 * HD1].rearrange("p t (h d) -> p t h d", d=HD1)
                kv = qkv1[:, :, H1 * HD1:QK].rearrange("p t (h d) -> p t h d", d=HD1)
                dve.tensor_tensor(qn1.rearrange("p t (h d) -> p t h d", d=HD1), qv,
                                  rn1[:, :, 0:H1].unsqueeze(3).to_broadcast([P, TILES, H1, HD1]), ALU.mult)
                kn_v = kn1.rearrange("p t (h r d) -> p t h r d", r=H1 // KV1, d=HD1)
                for r in range(H1 // KV1):
                    last = dve.tensor_tensor(kn_v[:, :, :, r, :], kv,
                                             rn1[:, :, H1:H1 + KV1].unsqueeze(3).to_broadcast([P, TILES, KV1, HD1]), ALU.mult)
                last.then_inc(qkn_ready, 1)
                dve.wait_ge(qkt_done, b + 1)
                split_qk(b * QKS + PAIRS)
                for j in range(2):
                    rnd = b * ROUNDS + PAIRS + j
                    for c in range(NCH):
                        reduce_chunk(rnd, c)
                    split_m(rnd)
                    copy_mrow(rnd)
                normalise(b * (PAIRS + 1) + PAIRS, y1t)
                assert chain.n == DVE_LINKS, chain.n

        @block.tensor
        def _(pe):
            mm = nc.tensor.matmul
            G = dict(skip_group_check=True)

            pe.wait_ge(w_loaded, W_LOADS)
            for i in range(NLIN):
                o = psum[:, 0:2, :].rearrange("p b n -> p (b n)")[:, i * D:(i + 1) * D]
                last = mm(o, la[:, i, :], lb[:, i, :], start=True, stop=True)
            last.then_inc(lora_done, 1)
            pe.wait_ge(const_ready, 1)
            pe.wait_ge(act_setup, 5)
            pe.wait_ge(dve_setup, 6)

            def transpose_rows(dst, src):
                for t in range(TILES):
                    last = nc.tensor.transpose(dst[:, t * P:(t + 1) * P], src[:, t, :], ident[:, :])
                return last

            def project_qk(n):
                pe.wait_ge(wst_ready, 2 * n + 2)
                for i, rb in enumerate((R0, R1)):
                    last = split_matmul(nc, rb, (wst_hi[:, i, :], wst_lo[:, i, :]), (xt_hi[:, :], xt_lo[:, :]), True, True)
                last.then_inc(qk_done, 1)

            def project_v(n, p):
                for t in range(TILES):
                    c = slice(t * P, (t + 1) * P)
                    last = split_matmul(nc, R2[:, c], (xt_hi[:, c], xt_lo[:, c]),
                                        (wqkv_hi[:, 2, p, :], wqkv_lo[:, 2, p, :]), True, True)
                last.then_inc(v_done, 1)

            def max_chunk(c, rows):
                rb = CHUNK_BANK[c]
                for i, (h, t, o) in enumerate(CHUNKS[c]):
                    r = rows[h]
                    w = P * (t + 1)
                    mm(rb[:, o:o + w], qk_hi[r, 0, t * P:(t + 1) * P], qk_hi[r, 1, 0:w], start=(i == 0), stop=False, **G)
                    last = mm(rb[:, o + w - P:o + w], identb[:, :], causal[:, :], start=False, stop=True, **G)
                last.then_inc(max_done, 1)

            def score_blocks(rnd, h, rows):
                r = rows[h]
                for j in (2, 0, 1, 3) if h == 0 else (0, 1, 3, 2):
                    first = (j, h) not in ((3, 0), (2, 1), (3, 1))
                    if (j, h) == (2, 1):
                        pe.wait_ge(shared_bank, rnd + 1)
                    o = SOFF[h][j]
                    k, q = slice(j * P, (j + 1) * P), slice(j * P, T)
                    last = split_matmul(nc, scores[:, o:o + T - j * P], (qk_hi[r, 1, k], qk_lo[r, 1, k]),
                                        (qk_hi[r, 0, q], qk_lo[r, 0, q]), first, False, **G)
                    if (j, h) == (2, 0):
                        last.then_inc(shared_bank, 1)

            def shift(blocks):
                for h, j in blocks:
                    o = SOFF[h][j]
                    last = mm(scores[:, o:o + T - j * P], msel[:, h, :], mrow[:, j * P:T], start=False, stop=True, **G)
                last.then_inc(scores_done, 1)

            def score_round(rnd, rows):
                score_blocks(rnd, 0, rows)
                pe.wait_ge(m_ready, 2 * rnd + 2)
                for t in range(TILES):
                    last = nc.tensor.transpose(R1.bitcast(BF16)[0:4, t * P:(t + 1) * P], msplit[:, t, :], identb[:, :])
                last.then_inc(mrow_done, 1)
                score_blocks(rnd, 1, rows)
                pe.wait_ge(mrow_ready, rnd + 1)
                shift([(0, 0), (0, 1), (0, 3), (0, 2), (1, 2)])
                shift([(1, 0), (1, 1), (1, 3)])

            def weigh_values(rnd, v, m, col0, j):
                pe.wait_ge(masked, 5 * rnd + 5)
                for k in range(TILES):
                    for h in range(2):
                        o = SOFF[h][k]
                        c = col0 + h * m
                        last = mm(R1[c:c + m, k * P:T], v(k, h), probs[j][:, o:o + T - k * P],
                                  start=(k == 0), stop=(k == TILES - 1), tile_position=(0, c), **G)
                return last

            def sum_probs(rnd, m, col0, j):
                pe.wait_ge(presum_step, 6 * rnd + 6)
                for h in range(2):
                    c = col0 + h * m
                    o = SOFF[h][0]
                    mm(R2[c:c + m, P:T], ones[:, 0:m], psums[j][:, h, P:T], start=True, stop=True, tile_position=(0, c), **G)
                for h in range(2):
                    c = col0 + h * m
                    o = SOFF[h][0]
                    last = mm(R2[c:c + m, 0:P], ones[:, 0:m], probs[j][:, o:o + P], start=False, stop=True, tile_position=(0, c), **G)
                return last

            ROWS0 = [slice(0, DQ), slice(DQ, 2 * DQ)]

            def v_of_pair(k, h):
                return v0[:, k, h * DQ:(h + 1) * DQ]

            def project_unit(u, n, s, wait_bank):
                pe.wait_ge(gst_ready, 2 * n + 2)
                if wait_bank:
                    pe.wait_ge(hm_ready, n - 1)
                for i in range(2):
                    split_matmul(nc, bank[3 * s + i], (gst_hi[:, s, i * P:(i + 1) * P], gst_lo[:, s, i * P:(i + 1) * P]),
                                 (xt_hi[:, :], xt_lo[:, :]), True, True)
                mm(bank[3 * s + 2], csel[:, u, :], combt[:, :], start=True, stop=True).then_inc(gu_done, 1)

            def unit_down(u, n, s):
                pe.wait_ge(hm_ready, n + 1)
                for t in range(TILES):
                    last = mm(R2[:, t * P:(t + 1) * P], hm[:, s, t * P:(t + 1) * P], down[:, u, :], start=False, stop=False, **G)
                last.then_inc(down_done, 1)

            with pe.Fori(0, B) as b:
                pe.wait_ge(row_ready, b * 2 + 1)
                transpose_rows(R0, xn).then_inc(tr_done, 1)
                pe.wait_ge(xt_lo_ready, b + 1)
                for t in range(TILES):
                    c = slice(t * P, (t + 1) * P)
                    last = split_matmul(nc, R1[:, t * E:(t + 1) * E], (xt_hi[:, c], xt_lo[:, c]), (rw_hi[:, :], rw_lo[:, :]), True, True)
                last.then_inc(logits_done, 1)
                pe.wait_ge(comb_ready, b + 1)
                for t in range(TILES):
                    last = nc.tensor.transpose(bank[0].bitcast(BF16)[:, t * P:(t + 1) * P], comb3[:, t, :], identb[:, :])
                last.then_inc(combt_done, 1)

                project_qk(b * PAIRS)
                pe.wait_ge(qk_split, b * 2 * QKS + 2)
                for c in range(NCH):
                    if c in PREV:
                        pe.wait_ge(max_read, b * ROUNDS * NCH + PREV[c] + 1)
                    max_chunk(c, ROWS0)
                    if c == NCH - 2:
                        pe.wait_ge(max_read, b * ROUNDS * NCH + 3)
                        project_v(b * PAIRS, 0)
                wait_alone(pe, combt_ready, b + 1)
                with pe.Fori(0, PAIRS - 1) as p:
                    rnd = b * ROUNDS + p
                    pair = b * PAIRS + p
                    nxt = (b * ROUNDS + p) * NCH + NCH
                    pe.wait_ge(max_read, nxt)
                    score_round(rnd, ROWS0)
                    project_qk(pair + 1)
                    pe.wait_ge(v_ready, pair + 1)
                    pe.wait_ge(qk_split, b * 2 * QKS + p * 2 + 4)
                    max_chunk(0, ROWS0)
                    max_chunk(1, ROWS0)
                    weigh_values(rnd, v_of_pair, DQ, 0, 0)
                    pe.wait_ge(max_read, nxt + 1)
                    max_chunk(2, ROWS0)
                    pe.wait_ge(max_read, nxt + 2)
                    max_chunk(3, ROWS0)
                    pe.wait_ge(max_read, nxt + 3)
                    sum_probs(rnd, DQ, 0, 0).then_inc(s_done, 1)
                    pe.wait_ge(max_read, nxt + 4)
                    max_chunk(4, ROWS0)
                    pe.wait_ge(y_ready, b * (PAIRS + 1) + p + 1)
                    project_v(pair + 1, p + 1)
                    pe.wait_ge(max_read, nxt + 5)
                    max_chunk(5, ROWS0)
                rnd = b * ROUNDS + PAIRS - 1
                pe.wait_ge(max_read, rnd * NCH + NCH)
                score_round(rnd, ROWS0)
                pe.wait_ge(v_ready, b * PAIRS + PAIRS)
                weigh_values(rnd, v_of_pair, DQ, 0, 0)
                sum_probs(rnd, DQ, 0, 0).then_inc(s_done, 1)

                project_unit(0, b * UNITS, 0, False)
                pe.wait_ge(y_ready, b * (PAIRS + 1) + PAIRS)
                mm(R2, ident[:, :], x_all[:, b, :, :].rearrange("p t d -> p (t d)"), start=True, stop=False, **G)
                for t in range(TILES):
                    for p in range(PAIRS):
                        last = mm(R2[:, t * P:(t + 1) * P], yt[:, p, t * P:(t + 1) * P], w_out0[:, p, :], start=False, stop=False, **G)
                last.then_inc(down_done, 1)
                project_unit(1, b * UNITS + 1, 1, False)
                unit_down(0, b * UNITS, 0)
                project_unit(2, b * UNITS + 2, 0, True)
                unit_down(1, b * UNITS + 1, 1)
                with pe.Fori(0, (UNITS - 3) // 2) as i:
                    for s in range(2):
                        n = b * UNITS + i * 2 + (s + 3)
                        project_unit(i * 2 + (s + 3), n, (s + 1) % 2, True)
                        unit_down(i * 2 + (s + 2), n - 1, s % 2)
                unit_down(UNITS - 1, b * UNITS + UNITS - 1, (UNITS - 1) % 2)

                pe.wait_ge(row_ready, b * 2 + 2)
                transpose_rows(R0, xn).then_inc(tr_done, 1)
                pe.wait_ge(ht_ready, b + 1)
                for t in range(TILES):
                    o = psum[:, 0:2, :].rearrange("p b n -> p (b n)")[:, t * QKV1:(t + 1) * QKV1]
                    last = mm(o, ht[:, t * P:(t + 1) * P], wqkv1[:, :], start=True, stop=True)
                last.then_inc(qkv1_done, 1)
                for k in range(BLOCKS):
                    mm(R0, ones[0:1, :], bias_row[0:1, 2 * k, :].unsqueeze(1).to_broadcast([1, TILES, D]), start=True, stop=False, **G)
                    if k:
                        pe.wait_ge(h_ready, b * (BLOCKS - 1) + k)
                    for t in range(TILES):
                        last = mm(R0[:, t * P:(t + 1) * P], ht[:, t * P:(t + 1) * P], lin[:, 2 * k, :], start=False, stop=True, **G)
                    last.then_inc(lin_done, 1)
                    pe.wait_ge(zn_ready, b * BLOCKS + k + 1)
                    transpose_rows(R1, zn).then_inc(znt_done, 1)
                    pe.wait_ge(gt_ready, b * BLOCKS + k + 1)
                    if k < BLOCKS - 1:
                        mm(R2, lin[:, 2 * k + 1, :], gt, start=True, stop=True).then_inc(f_done, 1)
                pe.wait_ge(qkn_ready, b + 1)
                transpose_rows(R0, qn1)
                transpose_rows(R1, kn1).then_inc(qkt_done, 1)
                pe.wait_ge(qk_split, b * 2 * QKS + 2 * QKS)
                for j in range(2):
                    rnd = b * ROUNDS + PAIRS + j
                    rows = [slice((2 * j + h) * HD1, (2 * j + h + 1) * HD1) for h in range(2)]
                    for c in range(NCH):
                        if c in PREV:
                            pe.wait_ge(max_read, rnd * NCH + PREV[c] + 1)
                        elif j == 1 and c == 0:
                            pe.wait_ge(max_read, rnd * NCH)
                            pe.wait_ge(mrow_ready, rnd)
                            pe.wait_ge(exp_done, 2 * rnd)
                        max_chunk(c, rows)
                    pe.wait_ge(max_read, rnd * NCH + NCH)
                    score_round(rnd, rows)
                for j in range(2):
                    rnd = b * ROUNDS + PAIRS + j
                    weigh_values(rnd, lambda k, h: qkv1[:, k, (H1 + KV1 + j) * HD1:(H1 + KV1 + j + 1) * HD1], HD1, 2 * j * HD1, j)
                for j in range(2):
                    rnd = b * ROUNDS + PAIRS + j
                    last = sum_probs(rnd, HD1, 2 * j * HD1, j)
                last.then_inc(s_done, 1)
                pe.wait_ge(xr_ready, b + 1)
                mm(bank[0], ident[:, :], xr.rearrange("p t d -> p (t d)"), start=True, stop=False, **G)
                mm(bank[0], ones[0:1, :], bias_row[0:1, NLIN - 1, :].unsqueeze(1).to_broadcast([1, TILES, D]), start=False, stop=False, **G)
                for t in range(TILES):
                    c = slice(t * P, (t + 1) * P)
                    mm(bank[0][:, c], ht[:, c], ident[:, :], start=False, stop=False, **G)
                    mm(bank[0][:, c], gt[:, c], lin[:, NLIN - 1, :], start=False, stop=False, **G)
                pe.wait_ge(y_ready, b * (PAIRS + 1) + PAIRS + 1)
                for t in range(TILES):
                    c = slice(t * P, (t + 1) * P)
                    last = mm(bank[0][:, c], y1t[:, c], wo1[:, :], start=False, stop=True, **G)
                last.then_inc(x2_done, 1)


def kernel(**inputs):
    import numpy as _np
    import concourse.bacc as _bacc
    from concourse import mybir as _mybir
    from concourse.bass_utils import run_bass_kernel_spmd as _run

    g = {k: _np.asarray(v) for k, v in inputs.items()}

    def heads_first(w):
        return w.transpose(1, 2, 0).reshape(D, H0 * DQ)

    gu = g["L0_ffn_gate_up_proj"].reshape(E // 2, 2, 2, I, D)
    gu = gu.transpose(4, 0, 2, 1, 3).reshape(D, E // 2, 2 * P)
    shared = _np.concatenate([g["L0_ffn_shared_gate_w"], g["L0_ffn_shared_up_w"]], 0).T.reshape(D, 1, 2 * P)
    dn = g["L0_ffn_down_proj"].transpose(0, 2, 1).reshape(E // 2, P, D).transpose(1, 0, 2)
    shared_dn = g["L0_ffn_shared_down_w"].T.reshape(P, 1, D)
    lay = {
        "x": g["L0_attn_x"],
        "wqkv": _np.concatenate([heads_first(g[f"L0_attn_{n}"]) for n in "QKV"], 1),
        "w_out0": g["L0_attn_W"].transpose(2, 1, 0).reshape(PAIRS, P, D).transpose(1, 0, 2),
        "router": g["L0_ffn_router_weight"].T,
        "ebias": g["L0_ffn_e_score_bias"],
        "gu": _np.concatenate([shared, gu], 1),
        "down": _np.concatenate([shared_dn, dn], 1),
        "wqkv1": _np.concatenate([g["L1_attn_Wq"], g["L1_attn_Wk"], g["L1_attn_Wv"]], 1),
        "norm_w": g["L1_attn_norm_w"].reshape(D, 1),
        "wo1": g["L1_attn_Wo"],
        "gate1": g["L1_attn_gate"].reshape(1),
        "temp1": g["L1_attn_log_temperature"].reshape(1),
        "qw": g["L1_ffn_qweights"].transpose(2, 0, 1),
        "qs": g["L1_ffn_scales"].transpose(2, 0, 1),
        "la": g["L1_ffn_lora_a"].transpose(1, 0, 2),
        "lb": g["L1_ffn_lora_b"].transpose(2, 0, 1),
        "bias_col": g["L1_ffn_biases"].T,
        "bias_row": g["L1_ffn_biases"].reshape(1, NLIN, D),
        "ln_g": g["L1_ffn_ln_gamma"].T,
        "ln_b": g["L1_ffn_ln_beta"].T,
    }
    nc = _bacc.Bacc("TRN2", target_bir_lowering=False, num_devices=1)
    arrays, args = {}, {}
    for name, v in lay.items():
        v = _np.ascontiguousarray(v)
        arrays[f"in_{name}"] = v
        args[name] = nc.dram_tensor(f"in_{name}", v.shape, _mybir.dt.from_np(v.dtype), kind="ExternalInput").ap()
    out = nc.dram_tensor("out_rows", (B, T, D), F32, kind="ExternalOutput").ap()
    build(nc, args, out)
    r = _run(nc, [arrays], core_ids=[0])
    return r.results[0]["out_rows"]
```

```python
from contextlib import ExitStack

import concourse.bass as bass
from concourse import mybir

F32 = mybir.dt.float32
F32R = mybir.dt.float32r
BF16 = mybir.dt.bfloat16
I32 = mybir.dt.int32
U32 = mybir.dt.uint32
ACT = mybir.ActivationFunctionType
ALU = mybir.AluOpType
AX = mybir.AxisListType.X

P = 128
B, T, D = 8, 512, 128
TILES = T // P
H0, DQ = 16, 64
PAIRS = H0 // 2
E, I, TOPK = 32, 64, 6
UNITS = 1 + E // 2
H1, KV1, HD1 = 4, 2, 32
QKV1 = (H1 + 2 * KV1) * HD1
R, GROUP, NLIN = 32, 16, 6
BLOCKS = NLIN // 2
EPS = 1e-5
EPS_RMS = 1e-6
EPS_L2 = 1e-12
NORM_MIN = 1e-12
NEG = -1e30
SCALE0 = (DQ / D) / DQ
OUT0 = 1.0 / H0
G = 4
ROUNDS0 = B * PAIRS
TT = B * TILES
LNS = 1 + BLOCKS

CHUNKS = [[(0, 3, 0)], [(1, 3, 0)], [(0, 2, 0), (0, 0, 384)], [(1, 2, 0), (1, 0, 384)], [(0, 1, 0)], [(1, 1, 0)]]
NCH = len(CHUNKS)
SLOT = {3: 0, 2: 1, 0: 2, 1: 3}
PROB = {3: 0, 2: 512, 0: 896, 1: 1024}
HALF = 1280


def split_matmul(nc, out, lhs, rhs, start, stop, **kw):
    (lh, ll), (rh, rl) = lhs, rhs
    nc.tensor.matmul(out, lh, rh, start=start, stop=False, **kw)
    nc.tensor.matmul(out, lh, rl, start=False, stop=False, **kw)
    return nc.tensor.matmul(out, ll, rh, start=False, stop=stop, **kw)


class Chain:

    def __init__(self, eng, sem, base):
        self.eng, self.sem, self.base, self.n = eng, sem, base, 0

    def step(self, ins):
        ins.then_inc(self.sem, 1)
        self.n += 1
        self.eng.wait_ge(self.sem, self.base + self.n)
        return self


def build(nc, a, out_dram):
    with ExitStack() as ctx:
        def sb(name, shape, dt=F32):
            return ctx.enter_context(nc.sbuf_tensor(name, shape, dt))

        def sem(name):
            return ctx.enter_context(nc.semaphore(name))

        x_all = sb("x_all", [P, B, TILES, D])
        wraw = sb("wraw", [P, UNITS, 2 * P])
        wqkv_raw = wraw[:, 0:12, :].rearrange("p u n -> p (u n)")
        wqkv_hi = sb("wqkv_hi", [P, 3, PAIRS, P], F32R)
        wqkv_lo = sb("wqkv_lo", [P, 3, PAIRS, P], F32R)
        gu_hi = sb("gu_hi", [P, UNITS, 2 * P], F32R)
        gu_lo = sb("gu_lo", [P, UNITS, 2 * P], F32R)
        down = sb("down", [P, UNITS, D])
        w_out0 = sb("w_out0", [P, PAIRS, D])
        rw_raw = sb("rw_raw", [P, E])
        rw_hi = sb("rw_hi", [P, E], F32R)
        rw_lo = sb("rw_lo", [P, E], F32R)
        ebias = sb("ebias", [P, E])
        wqkv1 = sb("wqkv1", [P, QKV1])
        norm_w = sb("norm_w", [P, 1])
        wo1 = sb("wo1", [P, D])
        gate1 = sb("gate1", [P, 1])
        temp1 = sb("temp1", [P, 2])
        lin = sb("lin", [P, NLIN, D])
        la = sb("la", [R, NLIN, D])
        lb = sb("lb", [R, NLIN, D])
        bias_col = sb("bias_col", [P, NLIN])
        bias_row = sb("bias_row", [1, NLIN, D])
        ln_g = sb("ln_g", [P, BLOCKS])
        ln_b = sb("ln_b", [P, BLOCKS])

        ident = sb("ident", [P, P])
        identb = sb("identb", [P, P], BF16)
        causal = sb("causal", [P, P], BF16)
        csel = sb("csel", [P, UNITS, P], BF16)
        ones = sb("ones", [1, P])
        mhalf = sb("mhalf", [P, TT])
        iota_e = sb("iota_e", [P, E])
        iota_i = sb("iota_i", [P, E], I32)

        stats = sb("stats", [P, TT, 6])
        mv = sb("mv", [P, TT, 2])
        var = sb("var", [P, TT])
        rstd = sb("rstd", [P, TT])
        xn = sb("xn", [P, TILES, D])
        xt_hi = sb("xt_hi", [P, T], F32R)
        xt_lo = sb("xt_lo", [P, T], F32R)
        wst_hi = sb("wst_hi", [P, 2, P], F32R)
        wst_lo = sb("wst_lo", [P, 2, P], F32R)
        qk_hi = sb("qk_hi", [P, 2, T], F32R)
        qk_lo = sb("qk_lo", [P, 2, T], F32R)
        v0 = sb("v0", [P, TILES, P])
        mneg = sb("mneg", [P, 2, TILES])
        rsum = sb("rsum", [P, 2, TILES])
        rinv = sb("rinv", [P, 2, TILES])
        probs = sb("probs", [P, 2 * HALF])
        pt = sb("pt", [P, 2, TILES, TILES, P])
        yt = sb("yt", [P, PAIRS, T])
        comb3 = sb("comb3", [P, TT, P], BF16)
        combt = sb("combt", [P, T], BF16)
        gst_hi = sb("gst_hi", [P, 2, 2 * P], F32R)
        gst_lo = sb("gst_lo", [P, 2, 2 * P], F32R)
        rsmall = sb("rsmall", [P, 2, TT])
        top8 = sb("top8", [P, TT, 8])
        idx8 = sb("idx8", [P, TT, 8], U32)
        idxf = sb("idxf", [P, TT, 8])

        stats_b = stats[:, :, :].rearrange("p (b t) s -> p b t s", t=TILES)
        mv_b = mv[:, :, :].rearrange("p (b t) s -> p b t s", t=TILES)
        rstd_b = rstd[:, :].rearrange("p (b t) -> p b t", t=TILES)
        comb3_b = comb3[:, :, :].rearrange("p (b t) e -> p b t e", t=TILES)

        flat_pt = pt[:, :, :, :, :].rearrange("p h j t q -> p (h j t q)")
        flat_yt = yt[:, :, :].rearrange("p n t -> p (n t)")
        qw = probs[:, 0:NLIN * D].rearrange("p (n d) -> p n d", n=NLIN).bitcast(I32)
        qs = probs[:, HALF:HALF + NLIN * D].rearrange("p (n d) -> p n d", n=NLIN)
        logits, rl, corr, comb = (flat_yt[:, n * TT * E:(n + 1) * TT * E].rearrange("p (t e) -> p t e", e=E) for n in range(4))
        logits_b = logits.rearrange("p (b t) e -> p b t e", t=TILES)
        HT = TT // 2
        onehot = flat_pt[:, 0:HT * E * TOPK].rearrange("p (t e k) -> p t e k", t=HT, e=E)
        sg = flat_pt[:, 0:2 * T].rearrange("p (s t) -> p s t", s=2)
        hm = flat_pt[:, 2 * T:4 * T].rearrange("p (s t) -> p s t", s=2)

        room = [gu_hi[:, :, :].bitcast(F32).rearrange("p u n -> p (u n)"), gu_lo[:, :, :].bitcast(F32).rearrange("p u n -> p (u n)"),
                flat_yt, wraw[:, :, :].rearrange("p u n -> p (u n)")]

        def rows(v):
            return v.rearrange("p (t n) -> p t n", t=TILES)

        xn1 = [rows(room[g][:, 0:T]) for g in range(G)]
        ht = [room[g][:, T:2 * T] for g in range(G)]
        gt = [room[g][:, 2 * T:3 * T] for g in range(G)]
        zn = [rows(room[g][:, 3 * T:4 * T]) for g in range(G)]
        qkv1 = [rows(room[g][:, 4 * T:6 * T]) for g in range(G)]
        kn1 = [rows(room[g][:, 6 * T:7 * T]) for g in range(G)]
        y1t = [room[g][:, 7 * T:8 * T] for g in range(G)]
        QK = (H1 + KV1) * HD1
        sq1 = [rows(room[g][:, 2 * T:2 * T + TILES * QK]) for g in range(G)]
        ss1 = sb("ss1", [P, G, TILES * (H1 + KV1)])
        rn1 = sb("rn1", [P, G, TILES * (H1 + KV1)])

        psum = ctx.enter_context(nc.psum_tensor("psum", [P, 8, 512], F32))
        bank = [psum[:, i, :] for i in range(8)]
        score_bank = bank[0:3]
        turn_bank = bank[3:5]
        Q0, Q1, Y = bank[5], bank[6], bank[7]
        ACC = Q1

        x_loaded = sem("x_loaded")
        qkvw_loaded = sem("qkvw_loaded")
        guw_loaded = sem("guw_loaded")
        w_loaded = sem("w_loaded")
        const_ready = sem("const_ready")
        pool_setup = sem("pool_setup")
        hi_setup = sem("hi_setup")
        lo_setup = sem("lo_setup")
        rw_hi_ready = sem("rw_hi_ready")
        rw_lo_ready = sem("rw_lo_ready")
        dve_setup = sem("dve_setup")
        act_setup = sem("act_setup")
        lora_done = sem("lora_done")
        dve_chain = sem("dve_chain")
        var_ready = sem("var_ready")
        rstd_ready = sem("rstd_ready")
        row_ready = sem("row_ready")
        tr_done = sem("tr_done")
        xt_hi_ready = sem("xt_hi_ready")
        xt_lo_ready = sem("xt_lo_ready")
        logits_done = sem("logits_done")
        rl_ready = sem("rl_ready")
        rexp_done = sem("rexp_done")
        comb_ready = sem("comb_ready")
        combt_done = sem("combt_done")
        combt_ready = sem("combt_ready")
        wst_ready = sem("wst_ready")
        qk_done = sem("qk_done")
        qk_hi_ready = sem("qk_hi_ready")
        qk_lo_ready = sem("qk_lo_ready")
        v_done = sem("v_done")
        v_ready = sem("v_ready")
        scored = sem("scored")
        max_ready = sem("max_ready")
        exp_done = sem("exp_done")
        rinv_ready = sem("rinv_ready")
        normed = sem("normed")
        turned = sem("turned")
        pt_ready = sem("pt_ready")
        y_done = sem("y_done")
        y_ready = sem("y_ready")
        gst_ready = sem("gst_ready")
        gu_done = sem("gu_done")
        silu_done = sem("silu_done")
        su_done = sem("su_done")
        hm_ready = sem("hm_ready")
        down_done = sem("down_done")
        rows_done = sem("rows_done")
        rows_ready = sem("rows_ready")
        ssq_ready = sem("ssq_ready")
        ms_ready = sem("ms_ready")
        rms_ready = sem("rms_ready")
        ht_ready = sem("ht_ready")
        qkv1_done = sem("qkv1_done")
        qkv1_ready = sem("qkv1_ready")
        ss1_ready = sem("ss1_ready")
        rn1_ready = sem("rn1_ready")
        qkn_ready = sem("qkn_ready")
        lin_done = sem("lin_done")
        zn_ready = sem("zn_ready")
        znt_done = sem("znt_done")
        gt_ready = sem("gt_ready")
        f_done = sem("f_done")
        h_ready = sem("h_ready")
        stored = sem("stored")
        waits_over = sem("waits_over")

        block = ctx.enter_context(nc.Block())

        def wait_alone(eng, s, value):
            eng.wait_ge(s, value)
            eng.sem_inc(waits_over, 1)

        x_v = a["x"].rearrange("b (t p) d -> b p t d", p=P)
        out_v = out_dram.rearrange("b (t p) d -> b p t d", p=P)
        GROUPS = B // G

        X_LOADS = 16 * (B + 1)

        @block.sync
        def _(sp):
            for i in range(B):
                sp.dma_start(x_all[:, i, :, :], x_v[i, :, :, :]).then_inc(x_loaded, 16)
            sp.dma_start(rw_raw[:, :], a["router"]).then_inc(x_loaded, 16)
            sp.dma_start(wqkv_raw, a["wqkv"]).then_inc(qkvw_loaded, 16)
            sp.wait_ge(lo_setup, 1)
            sp.dma_start(wraw[:, :, :], a["gu"]).then_inc(guw_loaded, 16)
            with sp.Fori(0, B) as b:
                dst = out_v[b, :, :, :]
                src = x_all[:, b, :, :]
                sp.wait_ge(rows_ready, b + (B + 1))
                sp.dma_start(dst, src).then_inc(stored, 16)
            sp.wait_ge(stored, 16 * B)

        small_loads = [
            (ebias[:, :], a["ebias"].partition_broadcast(P)),
            (w_out0[:, :, :], a["w_out0"]), (down[:, :, :], a["down"]),
            (wqkv1[:, :], a["wqkv1"]), (norm_w[:, :], a["norm_w"]), (wo1[:, :], a["wo1"]),
            (gate1[:, :], a["gate1"].partition_broadcast(P)), (temp1[:, 0:1], a["temp1"].partition_broadcast(P)),
            (qw, a["qw"]), (la[:, :, :], a["la"]), (lb[:, :, :], a["lb"]),
            (bias_col[:, :], a["bias_col"]), (ln_g[:, :], a["ln_g"]), (ln_b[:, :], a["ln_b"]),
            (bias_row[:, :, :], a["bias_row"]),
        ]
        small_loads += [(qs[g * GROUP:(g + 1) * GROUP, :, :], a["qs"][g, :, :].partition_broadcast(GROUP)) for g in range(D // GROUP)]
        W_LOADS = 16 * len(small_loads)

        @block.gpsimd
        def _(pool):
            setup = Chain(pool, pool_setup, 0)
            pool.memset(mhalf[:, :], -0.5).then_inc(pool_setup, 1)
            pool.memset(ident[:, :], 0.0).then_inc(pool_setup, 1)
            pool.memset(identb[:, :], 0.0).then_inc(pool_setup, 1)
            pool.memset(causal[:, :], 0.0).then_inc(pool_setup, 1)
            pool.memset(csel[:, :, :], 0.0).then_inc(pool_setup, 1)
            pool.memset(ones[:, :], 1.0).then_inc(pool_setup, 1)
            setup.n = 6
            setup.step(pool.memset(comb3[:, :, :], 0.0))
            pool.memset(comb3[:, :, 3 * E:3 * E + 1], 1.0).then_inc(pool_setup, 1)
            setup.n += 1
            for m in (ident, identb):
                setup.step(pool.affine_select(out=m[:, :], in_=m[:, :], compare_op=ALU.not_equal, fill=1.0, base=0,
                                              pattern=[[-1, P]], channel_multiplier=1))
            setup.step(pool.affine_select(out=causal[:, :], in_=causal[:, :], compare_op=ALU.is_ge, fill=NEG, base=0,
                                          pattern=[[-1, P]], channel_multiplier=1))
            pairs_v = csel[:, 1:UNITS, :].rearrange("p u (h m) -> p u h m", h=2)
            for part in range(3):
                setup.step(pool.affine_select(out=pairs_v, in_=pairs_v, compare_op=ALU.not_equal, fill=1.0,
                                              base=-E * part, pattern=[[-2, UNITS - 1], [-1, 2], [0, I]], channel_multiplier=1))
            setup.step(pool.affine_select(out=csel[:, 0, :], in_=csel[:, 0, :], compare_op=ALU.not_equal, fill=1.0,
                                          base=-3 * E, pattern=[[0, P]], channel_multiplier=1))
            setup.step(pool.iota(iota_i[:, :], pattern=[[1, E]], base=0, channel_multiplier=0))
            pool.tensor_copy(iota_e[:, :], iota_i[:, :]).then_inc(const_ready, 1)
            pool.wait_ge(const_ready, 1)
            pool.wait_ge(var_ready, 1)
            pool.tensor_tensor(rstd[:, :], var[:, :], mhalf[:, :], ALU.pow).then_inc(rstd_ready, 1)

            def stage_qk(n, p):
                pool.tensor_copy(wst_hi[:, :, :], wqkv_hi[:, 0:2, p, :]).then_inc(wst_ready, 1)
                pool.tensor_copy(wst_lo[:, :, :], wqkv_lo[:, 0:2, p, :]).then_inc(wst_ready, 1)

            def divide_by_sums(rnd):
                for c in range(NCH):
                    pool.wait_ge(rinv_ready, rnd * NCH + c + 1)
                    for h, t, _ in CHUNKS[c]:
                        w = P * (t + 1)
                        v = probs[:, h * HALF + PROB[t]:h * HALF + PROB[t] + w]
                        last = pool.tensor_tensor(v, v, rinv[:, h, SLOT[t]:SLOT[t] + 1].to_broadcast([P, w]), ALU.mult)
                    last.then_inc(normed, 1)

            def stage_gu(n, u, s):
                pool.tensor_copy(gst_hi[:, s, :], gu_hi[:, u, :]).then_inc(gst_ready, 1)
                pool.tensor_copy(gst_lo[:, s, :], gu_lo[:, u, :]).then_inc(gst_ready, 1)

            pool.wait_ge(lo_setup, 2)
            pool.wait_ge(hi_setup, 2)
            with pool.Fori(0, B) as b:
                stage_qk(b * PAIRS, 0)
                wait_alone(pool, qk_done, (b * PAIRS + 1) * 2)
                stage_qk(b * PAIRS + 1, 1)
                with pool.Fori(0, PAIRS - 2) as p:
                    divide_by_sums(b * PAIRS + p)
                    wait_alone(pool, qk_done, (b * PAIRS + p) * 2 + 4)
                    stage_qk(b * PAIRS + p + 2, p + 2)
                for s in range(2):
                    divide_by_sums(b * PAIRS + PAIRS - 2 + s)
                    stage_gu(b * UNITS + s, s, s)
                wait_alone(pool, gu_done, b * UNITS + 1)
                stage_gu(b * UNITS + 2, 2, 0)
                with pool.Fori(0, (UNITS - 3) // 2) as i:
                    for s in range(2):
                        wait_alone(pool, gu_done, b * UNITS + i * 2 + s + 2)
                        stage_gu(b * UNITS + i * 2 + s + 3, i * 2 + (s + 3), (s + 1) % 2)

            with pool.Fori(0, GROUPS) as q:
                def inv_sqrt(n):
                    pool.wait_ge(var_ready, q * LNS + n + 2)
                    for g in range(G):
                        s = slice(g * TILES, (g + 1) * TILES)
                        pool.tensor_tensor(rstd[:, s], var[:, s], mhalf[:, s], ALU.pow).then_inc(rstd_ready, 1)

                inv_sqrt(0)
                pool.wait_ge(ms_ready, q + 1)
                pool.tensor_tensor(rsmall[:, 0, 0:G * TILES], rsmall[:, 1, 0:G * TILES], mhalf[:, 0:G * TILES], ALU.pow).then_inc(rms_ready, 1)
                for g in range(G):
                    pool.wait_ge(ss1_ready, q * G + g + 1)
                    pool.tensor_tensor(rn1[:, g, :], ss1[:, g, :], mhalf[:, 0:TILES * (H1 + KV1)], ALU.pow).then_inc(rn1_ready, 1)
                for r in range(2 * G):
                    divide_by_sums(q * 2 * G + ROUNDS0 + r)
                for k in range(BLOCKS):
                    inv_sqrt(1 + k)

        @block.scalar
        def _(act):
            for dst, src in small_loads:
                act.dma_start(dst, src).then_inc(w_loaded, 16)
            act.wait_ge(x_loaded, X_LOADS)
            act.activation(rw_hi[:, :], rw_raw[:, :], ACT.Copy).then_inc(rw_hi_ready, 1)
            act.wait_ge(qkvw_loaded, 16)
            act.activation(wqkv_hi[:, :, :, :].rearrange("p a b n -> p (a b n)"), wqkv_raw, ACT.Copy).then_inc(hi_setup, 1)

            def copy_xt(n):
                act.wait_ge(tr_done, n + 1)
                act.activation(xt_hi[:, :], Y, ACT.Copy).then_inc(xt_hi_ready, 1)

            with act.Fori(0, B) as b:
                copy_xt(b)
            act.wait_ge(guw_loaded, 16)
            act.activation(gu_hi[:, :, :], wraw[:, :, :], ACT.Copy).then_inc(hi_setup, 1)
            act.wait_ge(rl_ready, 1)
            act.activation(corr, rl, ACT.Exp).then_inc(rexp_done, 1)
            act.wait_ge(w_loaded, W_LOADS)
            act.activation(w_out0[:, :, :], w_out0[:, :, :], ACT.Copy, scale=OUT0).then_inc(act_setup, 1)
            act.activation(wqkv1[:, :], wqkv1[:, :], ACT.Copy, scale=norm_w[:, 0:1]).then_inc(act_setup, 1)
            act.activation(wo1[:, :], wo1[:, :], ACT.Copy, scale=gate1[:, 0:1]).then_inc(act_setup, 1)
            act.activation(temp1[:, 1:2], temp1[:, 0:1], ACT.Exp).then_inc(act_setup, 1)

            def exps(rnd, value_copy=None):
                for c in range(NCH):
                    act.wait_ge(max_ready, rnd * NCH + c + 1)
                    for h, t, o in CHUNKS[c]:
                        w = P * (t + 1)
                        s = slice(SLOT[t], SLOT[t] + 1)
                        last = act.activation(probs[:, h * HALF + PROB[t]:h * HALF + PROB[t] + w], score_bank[c % 3][:, o:o + w],
                                              ACT.Exp, bias=mneg[:, h, s], accum_out=rsum[:, h, s])
                    last.then_inc(exp_done, 1)
                    if c == 2 and value_copy is not None:
                        copy_v(value_copy)

            def copy_v(n):
                act.wait_ge(v_done, n + 1)
                act.activation(v0[:, :, :].rearrange("p t n -> p (t n)"), Q0, ACT.Copy).then_inc(v_ready, 1)

            def split_qk(n, scale):
                act.wait_ge(qk_done, n * 2 + 1)
                act.activation(qk_hi[:, 0, :], Q0, ACT.Copy, scale=scale).then_inc(qk_hi_ready, 1)
                act.wait_ge(qk_done, n * 2 + 2)
                act.activation(qk_hi[:, 1, :], Q1, ACT.Copy).then_inc(qk_hi_ready, 1)

            def copy_y(n, dst):
                act.wait_ge(y_done, n + 1)
                act.activation(dst, Y, ACT.Copy).then_inc(y_ready, 1)

            def silu(n, s, wait_buffer):
                act.wait_ge(gu_done, n + 1)
                if wait_buffer:
                    act.wait_ge(hm_ready, n - 1)
                act.activation(sg[:, s, :], bank[3 * s], ACT.Silu).then_inc(silu_done, 1)

            def store_rows(n, src):
                act.activation(x_all[:, n, :, :].rearrange("p t d -> p (t d)"), src, ACT.Copy).then_inc(rows_ready, 1)

            with act.Fori(0, B) as b:
                copy_xt(b + B)
                split_qk(b * PAIRS, SCALE0)
                act.wait_ge(combt_done, b + 1)
                act.activation(combt[:, :], Y.bitcast(BF16)[:, 0:T], ACT.Copy).then_inc(combt_ready, 1)
                exps(b * PAIRS)
                split_qk(b * PAIRS + 1, SCALE0)
                with act.Fori(0, PAIRS - 2) as p:
                    pair = b * PAIRS + p
                    exps(pair + 1, pair)
                    split_qk(pair + 2, SCALE0)
                    copy_y(pair, yt[:, p, :])
                pair = b * PAIRS + PAIRS - 1
                exps(pair, pair - 1)
                copy_y(pair - 1, yt[:, PAIRS - 2, :])
                copy_v(pair)
                copy_y(pair, yt[:, PAIRS - 1, :])
                for u in range(3):
                    silu(b * UNITS + u, u % 2, u == 2)
                with act.Fori(0, (UNITS - 3) // 2) as i:
                    for s in range(2):
                        silu(b * UNITS + i * 2 + (s + 3), (s + 1) % 2, True)
                act.wait_ge(down_done, b * UNITS + UNITS)
                store_rows(b, ACC)

            with act.Fori(0, GROUPS) as q:
                n0 = q * G
                for g in range(G):
                    act.wait_ge(row_ready, n0 + 2 * B + g + 1)
                    for t in range(TILES):
                        last = act.activation(gt[g][:, t * P:(t + 1) * P], xn1[g][:, t, :], ACT.Square,
                                              accum_out=rsmall[:, 0, g * TILES + t:g * TILES + t + 1])
                    last.then_inc(ssq_ready, 1)
                    act.wait_ge(tr_done, n0 + 2 * B + g + 1)
                    act.activation(ht[g], bank[g], ACT.Copy).then_inc(ht_ready, 1)
                for g in range(G):
                    act.wait_ge(qkv1_done, n0 + g + 1)
                    s = 4 + 2 * (g % 2)
                    act.activation(qkv1[g].rearrange("p t n -> p (t n)"), psum[:, s:s + 2, :].rearrange("p b n -> p (b n)"),
                                   ACT.Copy).then_inc(qkv1_ready, 1)
                for r in range(2 * G):
                    if r == 0:
                        split_qk(n0 + ROUNDS0, 1.0)
                    exps(n0 * 2 + ROUNDS0 + r)
                    if r % 2 == 1 and r < 2 * G - 1:
                        split_qk(n0 + ROUNDS0 + (r + 1) // 2, 1.0)
                    if r % 2 == 0 and r:
                        copy_y(n0 * 2 + ROUNDS0 + r - 1, y1t[r // 2 - 1])
                copy_y(n0 * 2 + ROUNDS0 + 2 * G - 1, y1t[G - 1])
                for k in range(BLOCKS):
                    for g in range(G):
                        act.wait_ge(znt_done, (n0 * BLOCKS) + k * G + g + 1)
                        act.activation(gt[g], bank[4 + g], ACT.Gelu, scale=ln_g[:, k:k + 1], bias=ln_b[:, k:k + 1]).then_inc(gt_ready, 1)
                for g in range(G):
                    act.wait_ge(rows_done, n0 + g + 1)
                    store_rows(n0 + g, bank[g])

        GROUP_LINKS = 2 * LNS + 3 * G + 1

        @block.vector
        def _(dve):
            chain = Chain(dve, dve_chain, 0)
            dve.wait_ge(x_loaded, X_LOADS)
            with dve.Fori(0, B) as b:
                for t in range(TILES):
                    last = dve.bn_stats(stats_b[:, b, t, :], x_all[:, b, t, :])
                last.then_inc(dve_chain, 1)
            chain.n = B
            dve.wait_ge(dve_chain, B)
            for t in range(TT):
                last = dve.bn_aggr(mv[:, t, :], stats[:, t, :])
            chain.step(last)
            dve.tensor_scalar(var[:, :], mv[:, :, 1], EPS, None, ALU.add).then_inc(var_ready, 1)
            dve.wait_ge(rw_hi_ready, 1)
            dve.tensor_tensor(rw_lo[:, :], rw_raw[:, :], rw_hi[:, :].bitcast(F32), ALU.subtract).then_inc(rw_lo_ready, 1)
            dve.wait_ge(hi_setup, 1)
            dve.tensor_tensor(wqkv_lo[:, :, :, :].rearrange("p a b n -> p (a b n)"), wqkv_raw,
                              wqkv_hi[:, :, :, :].rearrange("p a b n -> p (a b n)").bitcast(F32), ALU.subtract).then_inc(lo_setup, 1)

            def norm_rows(b):
                for t in range(TILES):
                    last = dve.tensor_scalar(xn[:, t, :], x_all[:, b, t, :], mv_b[:, b, t, 0:1], rstd_b[:, b, t:t + 1],
                                             ALU.subtract, ALU.mult)
                last.then_inc(row_ready, 1)

            def split_xt(n):
                dve.wait_ge(xt_hi_ready, n + 1)
                dve.tensor_tensor(xt_lo[:, :], Y, xt_hi[:, :].bitcast(F32), ALU.subtract).then_inc(xt_lo_ready, 1)

            def take_logits(b):
                dve.wait_ge(logits_done, b + 1)
                dve.tensor_copy(logits_b[:, b, :, :], Q0[:, 0:TILES * E].rearrange("p (t e) -> p t e", e=E)).then_inc(dve_chain, 1)

            dve.wait_ge(rstd_ready, 1)
            norm_rows(0)
            with dve.Fori(0, B - 1) as b:
                wait_alone(dve, tr_done, b + 1)
                norm_rows(b + 1)
                split_xt(b)
                take_logits(b)
            split_xt(B - 1)
            take_logits(B - 1)
            chain.n += B
            dve.wait_ge(dve_chain, chain.n)
            def over_experts(v):
                return v.unsqueeze(2).to_broadcast([P, TT, E])

            sm, ri = rsmall[:, 0, :], rsmall[:, 1, :]
            chain.step(dve.tensor_reduce(sm, logits, AX, ALU.max, negate=True))
            dve.tensor_tensor(rl, logits, over_experts(sm), ALU.add).then_inc(rl_ready, 1)
            dve.wait_ge(hi_setup, 2)
            dve.tensor_tensor(gu_lo[:, :, :], wraw[:, :, :], gu_hi[:, :, :].bitcast(F32), ALU.subtract).then_inc(lo_setup, 1)
            dve.wait_ge(w_loaded, W_LOADS)
            dve.wait_ge(rexp_done, 1)
            chain.step(dve.tensor_reduce(sm, corr, AX, ALU.add))
            chain.step(dve.reciprocal(ri, sm))
            chain.step(dve.tensor_tensor(rl, corr, over_experts(ri), ALU.mult))
            chain.step(dve.tensor_tensor(corr, rl, ebias[:, :].unsqueeze(1).to_broadcast([P, TT, E]), ALU.add))
            for t in range(TT):
                last = dve.max(top8[:, t, :], corr[:, t, :])
            chain.step(last)
            for t in range(TT):
                last = dve.max_index(idx8[:, t, :], top8[:, t, :], corr[:, t, :])
            chain.step(last)
            chain.step(dve.tensor_copy(idxf[:, :, :], idx8[:, :, :]))
            dve.wait_ge(const_ready, 1)
            for half in range(2):
                for t in range(HT):
                    last = dve.tensor_tensor(onehot[:, t, :, :], iota_e[:, :].unsqueeze(2).to_broadcast([P, E, TOPK]),
                                             idxf[:, half * HT + t, 0:TOPK].unsqueeze(1).to_broadcast([P, E, TOPK]), ALU.is_equal)
                chain.step(last)
                chain.step(dve.tensor_reduce(comb[:, half * HT:(half + 1) * HT, :], onehot, AX, ALU.add))
            chain.step(dve.tensor_tensor(comb, comb, rl, ALU.mult))
            chain.step(dve.tensor_reduce(sm, comb, AX, ALU.add))
            chain.step(dve.tensor_scalar(sm, sm, NORM_MIN, None, ALU.max))
            chain.step(dve.reciprocal(ri, sm))
            chain.step(dve.tensor_tensor(comb, comb, over_experts(ri), ALU.mult))
            chain.step(dve.tensor_copy(comb3[:, :, 0:E], comb))
            chain.step(dve.tensor_tensor(comb, comb, comb3[:, :, 0:E], ALU.subtract))
            chain.step(dve.tensor_copy(comb3[:, :, E:2 * E], comb))
            dve.tensor_tensor(comb3[:, :, 2 * E:3 * E], comb, comb3[:, :, E:2 * E], ALU.subtract).then_inc(comb_ready, 1)
            dve.tensor_copy(lin[:, :, :], qw).then_inc(dve_setup, 1)
            dve.wait_ge(dve_setup, 1)
            dve.tensor_scalar(lin[:, :, :], lin[:, :, :], 1.0 / 7.5, -1.0, ALU.mult, ALU.add).then_inc(dve_setup, 1)
            dve.wait_ge(dve_setup, 2)
            dve.tensor_tensor(lin[:, :, :], lin[:, :, :], qs, ALU.mult).then_inc(dve_setup, 1)
            dve.wait_ge(dve_setup, 3)
            dve.wait_ge(lora_done, 1)
            lin_v = lin[:, :, :].rearrange("p i o -> p (i o)")
            dve.tensor_tensor(lin_v[:, 0:512], lin_v[:, 0:512], bank[0], ALU.add).then_inc(dve_setup, 1)
            dve.tensor_tensor(lin_v[:, 512:768], lin_v[:, 512:768], bank[1][:, 0:256], ALU.add).then_inc(dve_setup, 1)

            def split_qk(n, scale):
                dve.wait_ge(qk_hi_ready, n * 2 + 1)
                dve.scalar_tensor_tensor(qk_lo[:, 0, :], Q0, scale, qk_hi[:, 0, :].bitcast(F32),
                                         ALU.mult, ALU.subtract).then_inc(qk_lo_ready, 1)
                dve.wait_ge(qk_hi_ready, n * 2 + 2)
                dve.tensor_tensor(qk_lo[:, 1, :], Q1, qk_hi[:, 1, :].bitcast(F32), ALU.subtract).then_inc(qk_lo_ready, 1)

            def take_turned(rnd, c):
                dve.wait_ge(turned, rnd * NCH + c + 1)
                for h, t, o in CHUNKS[c]:
                    last = dve.tensor_copy(pt[:, h, 0:t + 1, t, :], turn_bank[c % 2][:, o:o + P * (t + 1)].rearrange("p (j q) -> p j q", q=P))
                last.then_inc(pt_ready, 1)

            def row_maxima(rnd, c):
                dve.wait_ge(scored, rnd * NCH + c + 1)
                for h, t, o in CHUNKS[c]:
                    last = dve.tensor_reduce(mneg[:, h, SLOT[t]:SLOT[t] + 1], score_bank[c % 3][:, o:o + P * (t + 1)], AX, ALU.max, negate=True)
                last.then_inc(max_ready, 1)

            def invert_sums(rnd, c):
                dve.wait_ge(exp_done, rnd * NCH + c + 1)
                h, s = CHUNKS[c][0][0], SLOT[CHUNKS[c][0][1]]
                s = slice(s, s + len(CHUNKS[c]))
                dve.reciprocal(rinv[:, h, s], rsum[:, h, s]).then_inc(rinv_ready, 1)

            LAG = 2

            def attend(turn, score):
                for c in range(NCH):
                    if turn is not None:
                        take_turned(turn, c)
                    if score is not None:
                        row_maxima(score, c)
                        if c >= LAG:
                            invert_sums(score, c - LAG)
                if score is not None:
                    for c in range(NCH - LAG, NCH):
                        invert_sums(score, c)

            def hidden(n, s, wait_buffer):
                dve.wait_ge(silu_done, n + 1)
                dve.tensor_tensor(sg[:, s, :], sg[:, s, :], bank[3 * s + 1], ALU.mult).then_inc(su_done, 1)
                dve.wait_ge(su_done, n + 1)
                if wait_buffer is not None:
                    dve.wait_ge(down_done, wait_buffer)
                dve.tensor_tensor(hm[:, s, :], sg[:, s, :], bank[3 * s + 2], ALU.mult).then_inc(hm_ready, 1)

            with dve.Fori(0, B) as b:
                wait_alone(dve, tr_done, b + B)
                norm_rows(b)
                split_xt(b + B)
                split_qk(b * PAIRS, SCALE0)
                attend(None, b * PAIRS)
                split_qk(b * PAIRS + 1, SCALE0)
                with dve.Fori(0, PAIRS - 2) as p:
                    pair = b * PAIRS + p
                    attend(pair, pair + 1)
                    split_qk(pair + 2, SCALE0)
                pair = b * PAIRS + PAIRS - 1
                attend(pair - 1, pair)
                attend(pair, None)
                for u in range(3):
                    hidden(b * UNITS + u, u % 2, b * UNITS + 1 if u == 2 else None)
                with dve.Fori(0, (UNITS - 3) // 2) as i:
                    for s in range(2):
                        hidden(b * UNITS + i * 2 + (s + 3), (s + 1) % 2, b * UNITS + i * 2 + (s + 2))

            setup_links = chain.n
            with dve.Fori(0, GROUPS) as q:
                n0 = q * G
                chain = Chain(dve, dve_chain, q * GROUP_LINKS + setup_links)

                def layer_norms(n, srcs, dsts, out_sem, ready=None):
                    for g in range(G):
                        if ready is not None:
                            dve.wait_ge(*ready(g))
                        for t in range(TILES):
                            last = dve.bn_stats(stats[:, g * TILES + t, :], srcs[g][:, t, :])
                    chain.step(last)
                    dve.sem_inc(waits_over, 1)
                    for t in range(G * TILES):
                        last = dve.bn_aggr(mv[:, t, :], stats[:, t, :])
                    chain.step(last)
                    dve.tensor_scalar(var[:, 0:G * TILES], mv[:, 0:G * TILES, 1], EPS, None, ALU.add).then_inc(var_ready, 1)
                    for g in range(G):
                        dve.wait_ge(rstd_ready, (q * LNS + n) * G + g + 2)
                        for t in range(TILES):
                            k = g * TILES + t
                            last = dve.tensor_scalar(dsts[g][:, t, :], srcs[g][:, t, :], mv[:, k, 0:1], rstd[:, k:k + 1],
                                                     ALU.subtract, ALU.mult)
                        last.then_inc(out_sem, 1)

                dve.wait_ge(rows_ready, n0 + B)
                layer_norms(0, [x_all[:, n0 + g, :, :] for g in range(G)], xn1, row_ready)
                dve.wait_ge(ssq_ready, n0 + G)
                dve.tensor_scalar(rsmall[:, 1, 0:G * TILES], rsmall[:, 0, 0:G * TILES], 1.0 / D, EPS_RMS, ALU.mult, ALU.add).then_inc(ms_ready, 1)
                dve.wait_ge(rms_ready, q + 1)
                for g in range(G):
                    dve.wait_ge(qkv1_ready, n0 + g + 1)
                    rms = rsmall[:, 0, g * TILES:(g + 1) * TILES]
                    chain.step(dve.tensor_tensor(qkv1[g], qkv1[g], rms.unsqueeze(2).to_broadcast([P, TILES, QKV1]), ALU.mult))
                    chain.step(dve.tensor_tensor(sq1[g], qkv1[g][:, :, 0:QK], qkv1[g][:, :, 0:QK], ALU.mult))
                    chain.step(dve.tensor_reduce(ss1[:, g, :].rearrange("p (t h) -> p t h", t=TILES), sq1[g].rearrange("p t (h d) -> p t h d", d=HD1), AX, ALU.add))
                    dve.tensor_scalar(ss1[:, g, :], ss1[:, g, :], EPS_L2 * EPS_L2, None, ALU.max).then_inc(ss1_ready, 1)
                dve.wait_ge(rn1_ready, n0 + G)
                rn_v = rn1[:, :, :].rearrange("p g (t h) -> p (g t) h", t=TILES)
                chain.step(dve.tensor_scalar(rn_v[:, :, 0:H1], rn_v[:, :, 0:H1], temp1[:, 1:2], None, ALU.mult))
                for g in range(G):
                    rn = rn1[:, g, :].rearrange("p (t h) -> p t h", t=TILES)
                    qv = qkv1[g][:, :, 0:H1 * HD1].rearrange("p t (h d) -> p t h d", d=HD1)
                    kv = qkv1[g][:, :, H1 * HD1:QK].rearrange("p t (h d) -> p t h d", d=HD1)
                    dve.tensor_tensor(qv, qv, rn[:, :, 0:H1].unsqueeze(3).to_broadcast([P, TILES, H1, HD1]), ALU.mult)
                    kn_v = kn1[g].rearrange("p t (h r d) -> p t h r d", r=H1 // KV1, d=HD1)
                    for r in range(H1 // KV1):
                        last = dve.tensor_tensor(kn_v[:, :, :, r, :], kv,
                                                 rn[:, :, H1:H1 + KV1].unsqueeze(3).to_broadcast([P, TILES, KV1, HD1]), ALU.mult)
                    last.then_inc(qkn_ready, 1)
                for r in range(2 * G + 1):
                    if r == 0:
                        split_qk(n0 + ROUNDS0, 1.0)
                    rnd = n0 * 2 + ROUNDS0 + r
                    attend(n0 * 2 + (ROUNDS0 + r - 1) if r else None, rnd if r < 2 * G else None)
                    if r % 2 == 1 and r < 2 * G - 1:
                        split_qk(n0 + ROUNDS0 + (r + 1) // 2, 1.0)
                for k in range(BLOCKS):
                    layer_norms(1 + k, [rows(bank[g]) for g in range(G)], zn, zn_ready,
                                lambda g: (lin_done, n0 * BLOCKS + k * G + g + 1))
                    if k < BLOCKS - 1:
                        for g in range(G):
                            dve.wait_ge(f_done, n0 * (BLOCKS - 1) + k * G + g + 1)
                            dve.scalar_tensor_tensor(ht[g], bank[g], bias_col[:, 2 * k + 1:2 * k + 2], ht[g],
                                                     ALU.add, ALU.add).then_inc(h_ready, 1)
                assert chain.n == GROUP_LINKS, chain.n

        @block.tensor
        def _(pe):
            mm = nc.tensor.matmul
            K = dict(skip_group_check=True)

            def transpose_rows(dst, src):
                for t in range(TILES):
                    last = nc.tensor.transpose(dst[:, t * P:(t + 1) * P], src[:, t, :], ident[:, :])
                return last

            pe.wait_ge(const_ready, 1)
            pe.wait_ge(rw_lo_ready, 1)
            with pe.Fori(0, B) as b:
                pe.wait_ge(row_ready, b + 1)
                transpose_rows(Y, xn).then_inc(tr_done, 1)
                pe.wait_ge(xt_lo_ready, b + 1)
                for t in range(TILES):
                    c = slice(t * P, (t + 1) * P)
                    last = split_matmul(nc, Q0[:, t * E:(t + 1) * E], (xt_hi[:, c], xt_lo[:, c]), (rw_hi[:, :], rw_lo[:, :]), True, True)
                last.then_inc(logits_done, 1)
            pe.wait_ge(w_loaded, W_LOADS)
            for i in range(NLIN):
                o = psum[:, 0:2, :].rearrange("p b n -> p (b n)")[:, i * D:(i + 1) * D]
                last = mm(o, la[:, i, :], lb[:, i, :], start=True, stop=True)
            last.then_inc(lora_done, 1)
            pe.wait_ge(act_setup, 4)
            pe.wait_ge(comb_ready, 1)
            pe.wait_ge(dve_setup, 5)
            pe.wait_ge(lo_setup, 2)

            def project_qk(n):
                pe.wait_ge(wst_ready, n * 2 + 2)
                for i, rb in enumerate((Q0, Q1)):
                    split_matmul(nc, rb, (wst_hi[:, i, :], wst_lo[:, i, :]), (xt_hi[:, :], xt_lo[:, :]), True, True).then_inc(qk_done, 1)

            def project_v(p):
                for t in range(TILES):
                    c = slice(t * P, (t + 1) * P)
                    last = split_matmul(nc, Q0[:, c], (xt_hi[:, c], xt_lo[:, c]),
                                        (wqkv_hi[:, 2, p, :], wqkv_lo[:, 2, p, :]), True, True)
                last.then_inc(v_done, 1)

            def score_chunk(rnd, c, head_rows, first_round):
                if c >= 3 or not first_round:
                    pe.wait_ge(exp_done, rnd * NCH + (c - 2))
                sc = score_bank[c % 3]
                for i, (h, t, o) in enumerate(CHUNKS[c]):
                    r = head_rows[h]
                    w = P * (t + 1)
                    qs_, ks = slice(t * P, (t + 1) * P), slice(0, w)
                    split_matmul(nc, sc[:, o:o + w], (qk_hi[r, 0, qs_], qk_lo[r, 0, qs_]), (qk_hi[r, 1, ks], qk_lo[r, 1, ks]), i == 0, False, **K)
                    last = mm(sc[:, o + w - P:o + w], identb[:, :], causal[:, :], start=False, stop=True, **K)
                last.then_inc(scored, 1)

            def turn_chunk(rnd, c):
                pe.wait_ge(normed, rnd * NCH + c + 1)
                if c >= 2:
                    pe.wait_ge(pt_ready, rnd * NCH + (c - 1))
                for h, t, o in CHUNKS[c]:
                    for j in range(t + 1):
                        s = h * HALF + PROB[t] + j * P
                        last = nc.tensor.transpose(turn_bank[c % 2][:, o + j * P:o + (j + 1) * P], probs[:, s:s + P], ident[:, :])
                last.then_inc(turned, 1)

            def attend(turn, score, head_rows, qk, first_round=False, value_pair=None):
                for c in range(NCH):
                    if turn is not None:
                        turn_chunk(turn, c)
                    if score is not None:
                        if c == 0:
                            pe.wait_ge(qk_lo_ready, qk * 2 + 2)
                        score_chunk(score, c, head_rows, first_round)
                    if c == 2 and value_pair is not None:
                        project_v(value_pair)

            def weigh_values(rnd, v, m, col0):
                pe.wait_ge(pt_ready, rnd * NCH + NCH)
                for k in range(TILES):
                    for h in range(2):
                        c = col0 + h * m
                        last = mm(Y[c:c + m, k * P:T], v(k, h), pt[:, h, k, k:TILES, :].rearrange("p t q -> p (t q)"),
                                  start=(k == 0), stop=(k == TILES - 1), tile_position=(0, c), **K)
                last.then_inc(y_done, 1)

            ROWS0 = [slice(0, DQ), slice(DQ, 2 * DQ)]

            def weigh_pair(n):
                pe.wait_ge(v_ready, n + 1)
                weigh_values(n, lambda k, h: v0[:, k, h * DQ:(h + 1) * DQ], DQ, 0)

            def project_unit(u, n, s, wait_bank):
                pe.wait_ge(gst_ready, 2 * n + 2)
                if wait_bank:
                    pe.wait_ge(hm_ready, n - 1)
                for i in range(2):
                    split_matmul(nc, bank[3 * s + i], (gst_hi[:, s, i * P:(i + 1) * P], gst_lo[:, s, i * P:(i + 1) * P]),
                                 (xt_hi[:, :], xt_lo[:, :]), True, True)
                mm(bank[3 * s + 2], csel[:, u, :], combt[:, :], start=True, stop=True).then_inc(gu_done, 1)

            def unit_down(u, n, s):
                pe.wait_ge(hm_ready, n + 1)
                for t in range(TILES):
                    last = mm(ACC[:, t * P:(t + 1) * P], hm[:, s, t * P:(t + 1) * P], down[:, u, :], start=False, stop=False, **K)
                return last.then_inc(down_done, 1)

            with pe.Fori(0, B) as b:
                pe.wait_ge(row_ready, b + (B + 1))
                transpose_rows(Y, xn).then_inc(tr_done, 1)
                pe.wait_ge(xt_lo_ready, b + (B + 1))
                project_qk(b * PAIRS)
                for t in range(TILES):
                    last = nc.tensor.transpose(Y.bitcast(BF16)[:, t * P:(t + 1) * P], comb3_b[:, b, t, :], identb[:, :])
                last.then_inc(combt_done, 1)
                attend(None, b * PAIRS, ROWS0, b * PAIRS, first_round=True)
                project_qk(b * PAIRS + 1)
                with pe.Fori(0, PAIRS - 2) as p:
                    pair = b * PAIRS + p
                    attend(pair, pair + 1, ROWS0, pair + 1, value_pair=p)
                    wait_alone(pe, v_ready, pair + 1)
                    project_qk(pair + 2)
                    weigh_pair(pair)
                pair = b * PAIRS + PAIRS - 1
                attend(pair - 1, pair, ROWS0, pair, value_pair=PAIRS - 2)
                weigh_pair(pair - 1)
                project_v(PAIRS - 1)
                attend(pair, None, None, None)
                pe.wait_ge(exp_done, b * (PAIRS * NCH) + (PAIRS * NCH))
                project_unit(0, b * UNITS, 0, False)
                mm(ACC, ident[:, :], x_all[:, b, :, :].rearrange("p t d -> p (t d)"), start=True, stop=False, **K)
                weigh_pair(pair)
                project_unit(1, b * UNITS + 1, 1, False)
                pe.wait_ge(y_ready, b * PAIRS + PAIRS)
                for t in range(TILES):
                    for p in range(PAIRS):
                        mm(ACC[:, t * P:(t + 1) * P], yt[:, p, t * P:(t + 1) * P], w_out0[:, p, :], start=False, stop=False, **K)
                unit_down(0, b * UNITS, 0)
                project_unit(2, b * UNITS + 2, 0, True)
                unit_down(1, b * UNITS + 1, 1)
                with pe.Fori(0, (UNITS - 3) // 2) as i:
                    for s in range(2):
                        n = b * UNITS + i * 2 + (s + 3)
                        project_unit(i * 2 + (s + 3), n, (s + 1) % 2, True)
                        unit_down(i * 2 + (s + 2), n - 1, s % 2)
                unit_down(UNITS - 1, b * UNITS + UNITS - 1, (UNITS - 1) % 2)

            with pe.Fori(0, GROUPS) as q:
                n0 = q * G
                for g in range(G):
                    pe.wait_ge(row_ready, n0 + 2 * B + g + 1)
                    transpose_rows(bank[g], xn1[g]).then_inc(tr_done, 1)
                for g in range(G):
                    pe.wait_ge(ht_ready, n0 + g + 1)
                    if g >= 2:
                        pe.wait_ge(qkv1_ready, n0 + g - 1)
                    s = 4 + 2 * (g % 2)
                    o = psum[:, s:s + 2, :].rearrange("p b n -> p (b n)")
                    for t in range(TILES):
                        last = mm(o[:, t * QKV1:(t + 1) * QKV1], ht[g][:, t * P:(t + 1) * P], wqkv1[:, :], start=True, stop=True)
                    last.then_inc(qkv1_done, 1)

                def turn_qk(g):
                    pe.wait_ge(qkn_ready, n0 + g + 1)
                    transpose_rows(Q0, qkv1[g][:, :, 0:H1 * HD1]).then_inc(qk_done, 1)
                    transpose_rows(Q1, kn1[g]).then_inc(qk_done, 1)

                def weigh_round(r):
                    g, j = r // 2, r % 2
                    v1 = (H1 + KV1 + j) * HD1
                    weigh_values(n0 * 2 + ROUNDS0 + r, lambda k, h: qkv1[g][:, k, v1:v1 + HD1], HD1, 2 * j * HD1)

                pe.wait_ge(qkv1_ready, n0 + G)
                turn_qk(0)
                for r in range(2 * G):
                    head_rows = [slice((2 * (r % 2) + h) * HD1, (2 * (r % 2) + h + 1) * HD1) for h in range(2)]
                    attend(n0 * 2 + (ROUNDS0 + r - 1) if r else None, n0 * 2 + ROUNDS0 + r, head_rows, n0 + (ROUNDS0 + r // 2),
                           first_round=(r == 0))
                    if r % 2 == 1 and r < 2 * G - 1:
                        turn_qk((r + 1) // 2)
                    if r:
                        weigh_round(r - 1)
                attend(n0 * 2 + (ROUNDS0 + 2 * G - 1), None, None, None)
                weigh_round(2 * G - 1)
                for k in range(BLOCKS):
                    for g in range(G):
                        if k:
                            pe.wait_ge(h_ready, n0 * (BLOCKS - 1) + (k - 1) * G + g + 1)
                        mm(bank[g], ones[0:1, :], bias_row[0:1, 2 * k, :].unsqueeze(1).to_broadcast([1, TILES, D]), start=True, stop=False, **K)
                        for t in range(TILES):
                            last = mm(bank[g][:, t * P:(t + 1) * P], ht[g][:, t * P:(t + 1) * P], lin[:, 2 * k, :], start=False, stop=True, **K)
                        last.then_inc(lin_done, 1)
                    if k == 0:
                        pe.wait_ge(y_ready, n0 + (ROUNDS0 + G))
                    for g in range(G):
                        pe.wait_ge(zn_ready, n0 * BLOCKS + k * G + g + 1)
                        transpose_rows(bank[4 + g], zn[g]).then_inc(znt_done, 1)
                    if k < BLOCKS - 1:
                        for g in range(G):
                            pe.wait_ge(gt_ready, n0 * BLOCKS + k * G + g + 1)
                            mm(bank[g], lin[:, 2 * k + 1, :], gt[g], start=True, stop=True).then_inc(f_done, 1)
                for g in range(G):
                    pe.wait_ge(gt_ready, n0 * BLOCKS + (BLOCKS - 1) * G + g + 1)
                    mm(bank[g], ident[:, :], x_all[:, n0 + g, :, :].rearrange("p t d -> p (t d)"), start=True, stop=False, **K)
                    mm(bank[g], ident[:, :], xn1[g].rearrange("p t d -> p (t d)"), start=False, stop=False, **K)
                    mm(bank[g], ones[0:1, :], bias_row[0:1, NLIN - 1, :].unsqueeze(1).to_broadcast([1, TILES, D]), start=False, stop=False, **K)
                    for t in range(TILES):
                        c = slice(t * P, (t + 1) * P)
                        mm(bank[g][:, c], ht[g][:, c], ident[:, :], start=False, stop=False, **K)
                        mm(bank[g][:, c], gt[g][:, c], lin[:, NLIN - 1, :], start=False, stop=False, **K)
                        last = mm(bank[g][:, c], y1t[g][:, c], wo1[:, :], start=False, stop=True, **K)
                    last.then_inc(rows_done, 1)


def kernel(**inputs):
    import numpy as _np
    import concourse.bacc as _bacc
    from concourse import mybir as _mybir
    from concourse.bass_utils import run_bass_kernel_spmd as _run

    g = {k: _np.asarray(v) for k, v in inputs.items()}

    def heads_first(w):
        return w.transpose(1, 2, 0).reshape(D, H0 * DQ)

    gu = g["L0_ffn_gate_up_proj"].reshape(E // 2, 2, 2, I, D)
    gu = gu.transpose(4, 0, 2, 1, 3).reshape(D, E // 2, 2 * P)
    shared = _np.concatenate([g["L0_ffn_shared_gate_w"], g["L0_ffn_shared_up_w"]], 0).T.reshape(D, 1, 2 * P)
    dn = g["L0_ffn_down_proj"].transpose(0, 2, 1).reshape(E // 2, P, D).transpose(1, 0, 2)
    shared_dn = g["L0_ffn_shared_down_w"].T.reshape(P, 1, D)
    lay = {
        "x": g["L0_attn_x"],
        "wqkv": _np.concatenate([heads_first(g[f"L0_attn_{n}"]) for n in "QKV"], 1),
        "w_out0": g["L0_attn_W"].transpose(2, 1, 0).reshape(PAIRS, P, D).transpose(1, 0, 2),
        "router": g["L0_ffn_router_weight"].T,
        "ebias": g["L0_ffn_e_score_bias"],
        "gu": _np.concatenate([shared, gu], 1),
        "down": _np.concatenate([shared_dn, dn], 1),
        "wqkv1": _np.concatenate([g["L1_attn_Wq"], g["L1_attn_Wk"], g["L1_attn_Wv"]], 1),
        "norm_w": g["L1_attn_norm_w"].reshape(D, 1),
        "wo1": g["L1_attn_Wo"],
        "gate1": g["L1_attn_gate"].reshape(1),
        "temp1": g["L1_attn_log_temperature"].reshape(1),
        "qw": g["L1_ffn_qweights"].transpose(2, 0, 1),
        "qs": g["L1_ffn_scales"].transpose(2, 0, 1),
        "la": g["L1_ffn_lora_a"].transpose(1, 0, 2),
        "lb": g["L1_ffn_lora_b"].transpose(2, 0, 1),
        "bias_col": g["L1_ffn_biases"].T,
        "bias_row": g["L1_ffn_biases"].reshape(1, NLIN, D),
        "ln_g": g["L1_ffn_ln_gamma"].T,
        "ln_b": g["L1_ffn_ln_beta"].T,
    }
    nc = _bacc.Bacc("TRN2", target_bir_lowering=False, num_devices=1)
    arrays, args = {}, {}
    for name, v in lay.items():
        v = _np.ascontiguousarray(v)
        arrays[f"in_{name}"] = v
        args[name] = nc.dram_tensor(f"in_{name}", v.shape, _mybir.dt.from_np(v.dtype), kind="ExternalInput").ap()
    out = nc.dram_tensor("out_rows", (B, T, D), F32, kind="ExternalOutput").ap()
    build(nc, args, out)
    r = _run(nc, [arrays], core_ids=[0])
    return r.results[0]["out_rows"]
```

```python
from contextlib import ExitStack

import concourse.bass as bass
from concourse import mybir

F32 = mybir.dt.float32
F32R = mybir.dt.float32r
BF16 = mybir.dt.bfloat16
I32 = mybir.dt.int32
U32 = mybir.dt.uint32
ACT = mybir.ActivationFunctionType
ALU = mybir.AluOpType
AX = mybir.AxisListType.X

P = 128
B, T, D = 8, 512, 128
TILES = T // P
H0, DQ = 16, 64
PAIRS = H0 // 2
E, I, TOPK = 32, 64, 6
UNITS = 1 + E // 2
H1, KV1, HD1 = 4, 2, 32
QKV1 = (H1 + 2 * KV1) * HD1
R, GROUP, NLIN = 32, 16, 6
BLOCKS = NLIN // 2
EPS = 1e-5
EPS_RMS = 1e-6
EPS_L2 = 1e-12
NORM_MIN = 1e-12
NEG = -1e30
GONE = -3e38
TAKEN = 3e38
SCALE0 = (DQ / D) / DQ
OUT0 = 1.0 / H0
G = 4
ROUNDS0 = B * PAIRS
TT = B * TILES
LNS = 1 + BLOCKS
STEPS = BLOCKS * G

CHUNKS = [[(0, 3, 0)], [(1, 3, 0)], [(0, 2, 0), (0, 0, 384)], [(1, 2, 0), (1, 0, 384)], [(0, 1, 0)], [(1, 1, 0)]]
NCH = len(CHUNKS)
VHALVES = H0 * DQ // 512
FILLS = TILES * VHALVES
SLOT = {3: 0, 2: 1, 0: 2, 1: 3}
PROB = {3: 0, 2: 512, 0: 896, 1: 1024}
HALF = 1280


def split_matmul(nc, out, lhs, rhs, start, stop, **kw):
    (lh, ll), (rh, rl) = lhs, rhs
    nc.tensor.matmul(out, lh, rh, start=start, stop=False, **kw)
    nc.tensor.matmul(out, lh, rl, start=False, stop=False, **kw)
    return nc.tensor.matmul(out, ll, rh, start=False, stop=stop, **kw)


class Chain:

    def __init__(self, eng, sem, base):
        self.eng, self.sem, self.base, self.n = eng, sem, base, 0

    def step(self, ins):
        ins.then_inc(self.sem, 1)
        self.n += 1
        self.eng.wait_ge(self.sem, self.base + self.n)
        return self


def build(nc, a, out_dram):
    with ExitStack() as ctx:
        def sb(name, shape, dt=F32):
            return ctx.enter_context(nc.sbuf_tensor(name, shape, dt))

        def sem(name):
            return ctx.enter_context(nc.semaphore(name))

        x_all = sb("x_all", [P, B, TILES, D])
        wraw = sb("wraw", [P, UNITS, 2 * P])
        wqkv_raw = wraw[:, 0:12, :].rearrange("p u n -> p (u n)")
        wqkv_hi = sb("wqkv_hi", [P, 3, PAIRS, P], F32R)
        wqkv_lo = sb("wqkv_lo", [P, 3, PAIRS, P], F32R)
        gu_hi = sb("gu_hi", [P, UNITS, 2 * P], F32R)
        gu_lo = sb("gu_lo", [P, UNITS, 2 * P], F32R)
        down = sb("down", [P, UNITS, D])
        w_out0 = sb("w_out0", [P, PAIRS, D])
        rw_raw = sb("rw_raw", [P, E])
        ebias = sb("ebias", [P, E])
        wqkv1 = sb("wqkv1", [P, QKV1])
        norm_w = sb("norm_w", [P, 1])
        wo1 = sb("wo1", [P, D])
        gate1 = sb("gate1", [P, 1])
        temp1 = sb("temp1", [P, 2])
        lin = sb("lin", [P, NLIN, D])
        la = sb("la", [R, NLIN, D])
        lb = sb("lb", [R, NLIN, D])
        bias_col = sb("bias_col", [P, NLIN])
        bias_bf = sb("bias_bf", [P, NLIN, D], BF16)
        bias_on = sb("bias_on", [P, P], BF16)
        ln_g = sb("ln_g", [P, BLOCKS])
        ln_b = sb("ln_b", [P, BLOCKS])

        ident = sb("ident", [P, P])
        identb = sb("identb", [P, P], BF16)
        causal = sb("causal", [P, P], BF16)
        csel = sb("csel", [P, UNITS, P], BF16)
        mhalf = sb("mhalf", [P, TT])

        stats = sb("stats", [P, TT, 6])
        mv = sb("mv", [P, TT, 2])
        var = sb("var", [P, TT])
        rstd = sb("rstd", [P, TT])
        xn = sb("xn", [P, TILES, D])
        xt_hi = sb("xt_hi", [P, T], F32R)
        xt_lo = sb("xt_lo", [P, T], F32R)
        wst_hi = sb("wst_hi", [P, 2, P], F32R)
        wst_lo = sb("wst_lo", [P, 2, P], F32R)
        qk_hi = sb("qk_hi", [P, 2, T], F32R)
        qk_lo = sb("qk_lo", [P, 2, T], F32R)
        v0 = sb("v0", [P, TILES, P])
        mneg = sb("mneg", [P, 2, TILES])
        rsum = sb("rsum", [P, 2, TILES])
        rinv = sb("rinv", [P, 2, TILES])
        probs = sb("probs", [P, 2 * HALF])
        pt = sb("pt", [P, 2, TILES, TILES, P])
        yt = sb("yt", [P, PAIRS, T])
        comb3 = sb("comb3", [P, TT, P], BF16)
        combt = sb("combt", [P, T], BF16)
        gst_hi = sb("gst_hi", [P, 2, 2 * P], F32R)
        gst_lo = sb("gst_lo", [P, 2, 2 * P], F32R)
        rsmall = sb("rsmall", [P, 2, TT])
        top8 = sb("top8", [P, TT, 8])

        mv_b = mv[:, :, :].rearrange("p (b t) s -> p b t s", t=TILES)
        rstd_b = rstd[:, :].rearrange("p (b t) -> p b t", t=TILES)
        comb3_b = comb3[:, :, :].rearrange("p (b t) e -> p b t e", t=TILES)

        flat_pt = pt[:, :, :, :, :].rearrange("p h j t q -> p (h j t q)")
        flat_yt = yt[:, :, :].rearrange("p n t -> p (n t)")
        qw = probs[:, 0:NLIN * D].rearrange("p (n d) -> p n d", n=NLIN).bitcast(I32)
        qs, bias_raw = (probs[:, k * NLIN * D:(k + 1) * NLIN * D].rearrange("p (n d) -> p n d", n=NLIN) for k in (1, 2))
        logits, rl, rexp, comb = (flat_yt[:, n * TT * E:(n + 1) * TT * E].rearrange("p (t e) -> p t e", e=E) for n in range(4))
        logits_b = logits.rearrange("p (b t) e -> p b t e", t=TILES)
        xn_setup = [flat_pt[:, s * T:(s + 1) * T].rearrange("p (t d) -> p t d", t=TILES) for s in range(2)]
        xt_setup = [flat_pt[:, (2 + s) * T:(3 + s) * T] for s in range(2)]
        corr = flat_pt[:, 4 * T:4 * T + TT * (E + 2)].rearrange("p (t e) -> p t e", e=E + 2)
        left = flat_pt[:, 0:TT * (E + 2)].rearrange("p (t e) -> p t e", e=E + 2)
        lora = flat_pt[:, 4 * T + TT * (E + 2):4 * T + TT * (E + 2) + NLIN * D]
        v_all = wraw[:, :, :].rearrange("p u n -> p (u n)")[:, 0:TILES * H0 * DQ].rearrange("p (t n) -> p t n", t=TILES)
        v_pairs = v_all.rearrange("p t (n m) -> p t n m", m=P)
        sg = probs[:, 0:2 * T].rearrange("p (s t) -> p s t", s=2)
        hm = probs[:, 2 * T:4 * T].rearrange("p (s t) -> p s t", s=2)

        room = [gu_hi[:, :, :].bitcast(F32).rearrange("p u n -> p (u n)"), gu_lo[:, :, :].bitcast(F32).rearrange("p u n -> p (u n)"),
                flat_yt, wraw[:, :, :].rearrange("p u n -> p (u n)")]

        def rows(v):
            return v.rearrange("p (t n) -> p t n", t=TILES)

        xn1 = [rows(room[g][:, 0:T]) for g in range(G)]
        ht = [room[g][:, T:2 * T] for g in range(G)]
        gt = [room[g][:, 2 * T:3 * T] for g in range(G)]
        zn = [rows(room[g][:, 3 * T:4 * T]) for g in range(G)]
        qkv1 = [rows(room[g][:, 4 * T:6 * T]) for g in range(G)]
        kn1 = [rows(room[g][:, 6 * T:7 * T]) for g in range(G)]
        y1t = [room[g][:, 7 * T:8 * T] for g in range(G)]
        QK = (H1 + KV1) * HD1
        sq1 = [rows(room[g][:, 6 * T:6 * T + TILES * QK]) for g in range(G)]
        table_out = sb("table_out", [P, 1])
        nmean = sb("nmean", [P, G * TILES])
        nmr = sb("nmr", [P, G * TILES])
        ss1 = sb("ss1", [P, G, TILES * (H1 + KV1)])
        rn1 = sb("rn1", [P, G, TILES * (H1 + KV1)])

        psum = ctx.enter_context(nc.psum_tensor("psum", [P, 8, 512], F32))
        bank = [psum[:, i, :] for i in range(8)]
        score_bank = bank[0:3]
        turn_bank = bank[3:5]
        Q0, Q1, Y = bank[5], bank[6], bank[7]
        ACC = Y
        UNIT_BANKS = [bank[0:3], [bank[3], bank[4], bank[6]]]

        x_loaded0 = sem("x_loaded0")
        x_loaded1 = sem("x_loaded1")
        qkvw_loaded = sem("qkvw_loaded")
        guw_loaded = sem("guw_loaded")
        w_loaded = sem("w_loaded")
        const_ready = sem("const_ready")
        pool_setup = sem("pool_setup")
        hi_setup = sem("hi_setup")
        lo_setup = sem("lo_setup")
        xt_copied = sem("xt_copied")
        act_setup = sem("act_setup")
        lora_done = sem("lora_done")
        lora_taken = sem("lora_taken")
        lin_ready = sem("lin_ready")
        dve_chain = sem("dve_chain")
        var_ready = sem("var_ready")
        rstd_ready = sem("rstd_ready")
        row_ready = sem("row_ready")
        odd_row_ready = sem("odd_row_ready")
        tr_done = sem("tr_done")
        xt_hi_ready = sem("xt_hi_ready")
        xt_lo_ready = sem("xt_lo_ready")
        logits_done = sem("logits_done")
        logits_taken = sem("logits_taken")
        rl_ready = sem("rl_ready")
        rexp_done = sem("rexp_done")
        comb_ready = sem("comb_ready")
        combt_done = sem("combt_done")
        combt_ready = sem("combt_ready")
        wst_ready = sem("wst_ready")
        qk_done = sem("qk_done")
        qk_hi_ready = sem("qk_hi_ready")
        qk_lo_ready = sem("qk_lo_ready")
        v_done = sem("v_done")
        v_taken = sem("v_taken")
        v_ready = sem("v_ready")
        scored = sem("scored")
        max_ready = sem("max_ready")
        exp_done = sem("exp_done")
        rinv_ready = sem("rinv_ready")
        normed = sem("normed")
        turned = sem("turned")
        pt_ready = sem("pt_ready")
        y_done = sem("y_done")
        y_ready = sem("y_ready")
        gst_ready = sem("gst_ready")
        gu_done = sem("gu_done")
        silu_done = sem("silu_done")
        su_done = sem("su_done")
        hm_ready = sem("hm_ready")
        down_done = sem("down_done")
        acc_done = sem("acc_done")
        xr_ready = sem("xr_ready")
        ffn_done = sem("ffn_done")
        ffn_ready = sem("ffn_ready")
        rows_done = sem("rows_done")
        rows_ready = sem("rows_ready")
        nmr_ready = sem("nmr_ready")
        ms_ready = sem("ms_ready")
        rms_ready = sem("rms_ready")
        ht_ready = sem("ht_ready")
        qkv1_done = sem("qkv1_done")
        qkv1_ready = sem("qkv1_ready")
        ss1_ready = sem("ss1_ready")
        rn1_ready = sem("rn1_ready")
        qkn_ready = sem("qkn_ready")
        lin_done = sem("lin_done")
        zn_ready = sem("zn_ready")
        znt_done = sem("znt_done")
        gt_ready = sem("gt_ready")
        f_done = sem("f_done")
        h_ready = sem("h_ready")
        stored = sem("stored")
        waits_over = sem("waits_over")

        block = ctx.enter_context(nc.Block())

        def wait_alone(eng, s, value):
            eng.wait_ge(s, value)
            eng.sem_inc(waits_over, 1)

        x_v = a["x"].rearrange("b (t p) d -> b p t d", p=P)
        out_v = out_dram.rearrange("b (t p) d -> b p t d", p=P)
        GROUPS = B // G

        X_LOADS = 16 * (B // 2)

        @block.sync
        def _(sp):
            for i in range(B):
                sp.dma_start(x_all[:, i, :, :], x_v[i, :, :, :]).then_inc(x_loaded0 if i < B // 2 else x_loaded1, 16)
            sp.dma_start(rw_raw[:, :], a["router"]).then_inc(x_loaded1, 16)
            sp.dma_start(wqkv_raw, a["wqkv"]).then_inc(qkvw_loaded, 16)
            sp.wait_ge(lo_setup, 1)
            sp.dma_start(wraw[:, :, :], a["gu"]).then_inc(guw_loaded, 16)
            with sp.Fori(0, B) as b:
                dst = out_v[b, :, :, :]
                src = x_all[:, b, :, :]
                sp.wait_ge(rows_ready, b + (B + 1))
                sp.dma_start(dst, src).then_inc(stored, 16)
            sp.wait_ge(stored, 16 * B)

        small_loads = [
            (ebias[:, :], a["ebias"].partition_broadcast(P)),
            (w_out0[:, :, :], a["w_out0"]), (down[:, :, :], a["down"]),
            (wqkv1[:, :], a["wqkv1"]), (norm_w[:, :], a["norm_w"]), (wo1[:, :], a["wo1"]),
            (gate1[:, :], a["gate1"].partition_broadcast(P)), (temp1[:, 0:1], a["temp1"].partition_broadcast(P)),
            (qw, a["qw"]), (la[:, :, :], a["la"]), (lb[:, :, :], a["lb"]),
            (bias_col[:, :], a["bias_col"]), (ln_g[:, :], a["ln_g"]), (ln_b[:, :], a["ln_b"]),
            (bias_raw, a["bias_row"].partition_broadcast(P)),
        ]
        small_loads += [(qs[g * GROUP:(g + 1) * GROUP, :, :], a["qs"][g, :, :].partition_broadcast(GROUP)) for g in range(D // GROUP)]
        W_LOADS = 16 * len(small_loads)

        @block.gpsimd
        def _(pool):
            setup = Chain(pool, pool_setup, 0)
            pool.memset(mhalf[:, :], -0.5).then_inc(pool_setup, 1)
            pool.memset(ident[:, :], 0.0).then_inc(pool_setup, 1)
            pool.memset(identb[:, :], 0.0).then_inc(pool_setup, 1)
            pool.memset(causal[:, :], 0.0).then_inc(pool_setup, 1)
            pool.memset(csel[:, :, :], 0.0).then_inc(pool_setup, 1)
            pool.memset(bias_on[:, :], 0.0).then_inc(pool_setup, 1)
            setup.n = 6
            setup.step(pool.memset(comb3[:, :, :], 0.0))
            pool.memset(comb3[:, :, 3 * E:3 * E + 1], 1.0).then_inc(pool_setup, 1)
            setup.n += 1
            for m in (ident, identb):
                setup.step(pool.affine_select(out=m[:, :], in_=m[:, :], compare_op=ALU.not_equal, fill=1.0, base=0,
                                              pattern=[[-1, P]], channel_multiplier=1))
            for part in range(3):
                setup.step(pool.memset(bias_on[32 * part:32 * part + 1, :], 1.0))
            setup.step(pool.affine_select(out=causal[:, :], in_=causal[:, :], compare_op=ALU.is_ge, fill=NEG, base=0,
                                          pattern=[[-1, P]], channel_multiplier=1))
            pairs_v = csel[:, 1:UNITS, :].rearrange("p u (h m) -> p u h m", h=2)
            for part in range(3):
                setup.step(pool.affine_select(out=pairs_v, in_=pairs_v, compare_op=ALU.not_equal, fill=1.0,
                                              base=-E * part, pattern=[[-2, UNITS - 1], [-1, 2], [0, I]], channel_multiplier=1))
            setup.step(pool.affine_select(out=csel[:, 0, :], in_=csel[:, 0, :], compare_op=ALU.not_equal, fill=1.0,
                                          base=-3 * E, pattern=[[0, P]], channel_multiplier=1))
            pool.memset(corr[:, :, E:E + 2], GONE).then_inc(const_ready, 1)
            pool.wait_ge(const_ready, 1)
            pool.wait_ge(var_ready, 1)
            for b in range(B):
                s = slice(b * TILES, (b + 1) * TILES)
                pool.tensor_tensor(rstd[:, s], var[:, s], mhalf[:, s], ALU.pow).then_inc(rstd_ready, 1)

            def stage_qk(n, p):
                pool.tensor_copy(wst_hi[:, :, :], wqkv_hi[:, 0:2, p, :]).then_inc(wst_ready, 1)
                pool.tensor_copy(wst_lo[:, :, :], wqkv_lo[:, 0:2, p, :]).then_inc(wst_ready, 1)

            def divide_by_sums(rnd):
                for c in range(NCH):
                    pool.wait_ge(rinv_ready, rnd * NCH + c + 1)
                    for h, t, _ in CHUNKS[c]:
                        w = P * (t + 1)
                        v = probs[:, h * HALF + PROB[t]:h * HALF + PROB[t] + w]
                        last = pool.tensor_tensor(v, v, rinv[:, h, SLOT[t]:SLOT[t] + 1].to_broadcast([P, w]), ALU.mult)
                    last.then_inc(normed, 1)

            def stage_gu(n, u, s):
                pool.tensor_copy(gst_hi[:, s, :], gu_hi[:, u, :]).then_inc(gst_ready, 1)
                pool.tensor_copy(gst_lo[:, s, :], gu_lo[:, u, :]).then_inc(gst_ready, 1)

            def stage_first(b):
                stage_qk(b * PAIRS, 0)
                wait_alone(pool, qk_done, (b * PAIRS + 1) * 2)
                stage_qk(b * PAIRS + 1, 1)

            def first_layer(b):
                with pool.Fori(0, PAIRS - 2) as p:
                    divide_by_sums(b * PAIRS + p)
                    wait_alone(pool, qk_done, (b * PAIRS + p) * 2 + 4)
                    stage_qk(b * PAIRS + p + 2, p + 2)
                for s in range(2):
                    divide_by_sums(b * PAIRS + PAIRS - 2 + s)
                    stage_gu(b * UNITS + s, s, s)
                wait_alone(pool, gu_done, b * UNITS + 1)
                stage_gu(b * UNITS + 2, 2, 0)
                with pool.Fori(0, (UNITS - 3) // 2) as i:
                    for s in range(2):
                        wait_alone(pool, gu_done, b * UNITS + i * 2 + s + 2)
                        stage_gu(b * UNITS + i * 2 + s + 3, i * 2 + (s + 3), (s + 1) % 2)

            pool.wait_ge(w_loaded, W_LOADS)
            for part in range(3):
                rest = slice(32 * part, 32 * part + 32) if part else slice(0, P)
                for k in range(part):
                    if k:
                        setup.step(pool.tensor_copy(bias_bf[rest, :, :], bias_raw[rest, :, :]))
                    setup.step(pool.tensor_tensor(bias_raw[rest, :, :], bias_raw[rest, :, :], bias_bf[rest, :, :], ALU.subtract))
                setup.step(pool.tensor_copy(bias_bf[rest, :, :], bias_raw[rest, :, :]))
            pool.wait_ge(lo_setup, 1)
            stage_qk(0, 0)
            pool.wait_ge(w_loaded, W_LOADS)
            setup.step(pool.tensor_copy(lin[:, :, :], qw))
            setup.step(pool.tensor_scalar(lin[:, :, :], lin[:, :, :], 1.0 / 7.5, -1.0, ALU.mult, ALU.add))
            setup.step(pool.tensor_tensor(lin[:, :, :], lin[:, :, :], qs, ALU.mult))
            pool.wait_ge(hi_setup, 2)
            pool.tensor_tensor(gu_lo[:, :, :], wraw[:, :, :], gu_hi[:, :, :].bitcast(F32), ALU.subtract).then_inc(lo_setup, 1)
            pool.wait_ge(lora_taken, 2)
            pool.tensor_tensor(lin[:, :, :].rearrange("p i o -> p (i o)"), lin[:, :, :].rearrange("p i o -> p (i o)"), lora,
                               ALU.add).then_inc(lin_ready, 1)
            pool.wait_ge(qk_done, 2)
            stage_qk(1, 1)
            pool.wait_ge(lo_setup, 2)
            with pool.Fori(0, B - 1) as b:
                first_layer(b)
                stage_first(b + 1)
            first_layer(B - 1)

            with pool.Fori(0, GROUPS) as q:
                n0 = q * G

                def inv_sqrt(n, g):
                    pool.wait_ge(var_ready, q * LNS * G + n + 2)
                    s = slice(g * TILES, (g + 1) * TILES)
                    pool.tensor_tensor(rstd[:, s], var[:, s], mhalf[:, s], ALU.pow).then_inc(rstd_ready, 1)
                    pool.wait_ge(rstd_ready, q * LNS * G + (B + n + 1))
                    pool.tensor_tensor(nmr[:, s], nmean[:, s], rstd[:, s], ALU.mult).then_inc(nmr_ready, 1)

                def inv_norms(k):
                    g, t = k // TILES, k % TILES
                    c = slice(t * (H1 + KV1), (t + 1) * (H1 + KV1))
                    pool.wait_ge(ss1_ready, n0 + g + 1)
                    last = pool.tensor_tensor(rn1[:, g, c], ss1[:, g, c], mhalf[:, 0:H1 + KV1], ALU.pow)
                    if t == TILES - 1:
                        last.then_inc(rn1_ready, 1)

                for g in range(G):
                    inv_sqrt(g, g)
                pool.wait_ge(ms_ready, q + 1)
                for g in range(G):
                    s = slice(g * TILES, (g + 1) * TILES)
                    pool.tensor_tensor(rsmall[:, 0, s], rsmall[:, 1, s], mhalf[:, s], ALU.pow).then_inc(rms_ready, 1)
                for i in range(STEPS):
                    inv_sqrt(G + i, i % G)
                    for k in range(G * TILES):
                        if 1 + k * (STEPS - 2) // (G * TILES) == i:
                            inv_norms(k)
                for r in range(2 * G):
                    divide_by_sums(q * 2 * G + ROUNDS0 + r)

        @block.scalar
        def _(act):
            for dst, src in small_loads:
                act.dma_start(dst, src).then_inc(w_loaded, 16)
            act.wait_ge(qkvw_loaded, 16)
            act.activation(wqkv_hi[:, :, :, :].rearrange("p a b n -> p (a b n)"), wqkv_raw, ACT.Copy).then_inc(hi_setup, 1)

            with act.Fori(0, B // 2) as i:
                for s in range(2):
                    act.wait_ge(tr_done, i * 2 + s + 1)
                    act.activation(xt_setup[s], bank[s], ACT.Copy).then_inc(xt_copied, 1)
            act.wait_ge(guw_loaded, 16)
            act.activation(gu_hi[:, :, :], wraw[:, :, :], ACT.Copy).then_inc(hi_setup, 1)
            act.wait_ge(w_loaded, W_LOADS)
            act.activation(w_out0[:, :, :], w_out0[:, :, :], ACT.Copy, scale=OUT0).then_inc(act_setup, 1)
            act.activation(wqkv1[:, :], wqkv1[:, :], ACT.Copy, scale=norm_w[:, 0:1]).then_inc(act_setup, 1)
            act.activation(wo1[:, :], wo1[:, :], ACT.Copy, scale=gate1[:, 0:1]).then_inc(act_setup, 1)
            act.activation(temp1[:, 1:2], temp1[:, 0:1], ACT.Exp).then_inc(act_setup, 1)
            act.wait_ge(lora_done, 1)
            act.activation(lora[:, 0:512], bank[6], ACT.Copy).then_inc(lora_taken, 1)
            act.activation(lora[:, 512:NLIN * D], bank[7][:, 0:NLIN * D - 512], ACT.Copy).then_inc(lora_taken, 1)

            def copy_xt(n):
                act.wait_ge(tr_done, n + (B + 1))
                act.activation(xt_hi[:, :], Q0, ACT.Copy).then_inc(xt_hi_ready, 1)

            def exps(rnd, middle=None):
                for c in range(NCH):
                    act.wait_ge(max_ready, rnd * NCH + c + 1)
                    for h, t, o in CHUNKS[c]:
                        w = P * (t + 1)
                        s = slice(SLOT[t], SLOT[t] + 1)
                        last = act.activation(probs[:, h * HALF + PROB[t]:h * HALF + PROB[t] + w], score_bank[c % 3][:, o:o + w],
                                              ACT.Exp, bias=mneg[:, h, s], accum_out=rsum[:, h, s])
                    last.then_inc(exp_done, 1)
                    if c == 2 and middle is not None:
                        middle()

            def take_values(b):
                for f in range(FILLS):
                    t, half = f // VHALVES, f % VHALVES
                    act.wait_ge(v_done, b * FILLS + f + 1)
                    act.activation(v_all[:, t, half * 512:(half + 1) * 512], bank[3 + f % 2], ACT.Copy).then_inc(v_taken, 1)

            def stage_v(n, p):
                act.activation(v0[:, :, :], v_pairs[:, :, p, :], ACT.Copy).then_inc(v_ready, 1)

            def split_qk(n, scale):
                act.wait_ge(qk_done, n * 2 + 1)
                act.activation(qk_hi[:, 0, :], Q0, ACT.Copy, scale=scale).then_inc(qk_hi_ready, 1)
                act.wait_ge(qk_done, n * 2 + 2)
                act.activation(qk_hi[:, 1, :], Q1, ACT.Copy).then_inc(qk_hi_ready, 1)

            def copy_y(n, dst):
                act.wait_ge(y_done, n + 1)
                act.activation(dst, Y, ACT.Copy).then_inc(y_ready, 1)

            def silu(n, s, wait_buffer):
                act.wait_ge(gu_done, n + 1)
                if wait_buffer:
                    act.wait_ge(hm_ready, n - 1)
                act.activation(sg[:, s, :], UNIT_BANKS[s][0], ACT.Silu).then_inc(silu_done, 1)

            def load_table(func):
                act.activation(table_out[:, :], ln_g[:, 0:1], func)

            def store_rows(n, src):
                act.activation(x_all[:, n, :, :].rearrange("p t d -> p (t d)"), src, ACT.Copy).then_inc(rows_ready, 1)

            def copy_combt(b):
                act.wait_ge(combt_done, b + 1)
                act.activation(combt[:, :], Q0.bitcast(BF16)[:, 0:T], ACT.Copy).then_inc(combt_ready, 1)

            def first_pair(b):
                take_values(b)
                act.wait_ge(v_taken, b * FILLS + FILLS)
                stage_v(b * PAIRS, 0)
                exps(b * PAIRS)
                split_qk(b * PAIRS + 1, SCALE0)

            def first_layer(b):
                with act.Fori(0, PAIRS - 2) as p:
                    pair = b * PAIRS + p
                    exps(pair + 1)
                    split_qk(pair + 2, SCALE0)
                    copy_y(pair, yt[:, p, :])
                    stage_v(pair + 1, p + 1)
                pair = b * PAIRS + PAIRS - 1
                exps(pair)
                copy_y(pair - 1, yt[:, PAIRS - 2, :])
                stage_v(pair, PAIRS - 1)
                copy_combt(b)
                act.wait_ge(turned, pair * NCH + NCH)
                silu(b * UNITS, 0, False)
                copy_y(pair, yt[:, PAIRS - 1, :])
                silu(b * UNITS + 1, 1, False)
                silu(b * UNITS + 2, 0, True)
                with act.Fori(0, (UNITS - 3) // 2) as i:
                    for s in range(2):
                        silu(b * UNITS + i * 2 + (s + 3), (s + 1) % 2, True)

            def take_rows(b):
                act.wait_ge(acc_done, b + 1)
                store_rows(b, ACC)

            copy_xt(0)
            act.wait_ge(rl_ready, 1)
            act.activation(rexp, rl, ACT.Exp).then_inc(rexp_done, 1)
            split_qk(0, SCALE0)
            act.wait_ge(lo_setup, 2)
            act.wait_ge(lin_ready, 1)
            first_pair(0)
            with act.Fori(0, B - 1) as b:
                first_layer(b)
                copy_xt(b + 1)
                split_qk((b + 1) * PAIRS, SCALE0)
                first_pair(b + 1)
                take_rows(b)
            first_layer(B - 1)
            load_table(ACT.Gelu)
            take_rows(B - 1)

            with act.Fori(0, GROUPS) as q:
                n0 = q * G
                def norm_rows1(n, g, src, dst, out_sem):
                    act.wait_ge(nmr_ready, q * LNS * G + n + 1)
                    for t in range(TILES):
                        k = g * TILES + t
                        last = act.activation(dst[:, t, :], src[:, t, :], ACT.Identity, scale=rstd[:, k:k + 1], bias=nmr[:, k:k + 1])
                    last.then_inc(out_sem, 1)

                for g in range(G + 1):
                    if g < G and g % 2 == 0:
                        norm_rows1(g, g, x_all[:, n0 + g, :, :], xn1[g], row_ready)
                    if g:
                        act.wait_ge(tr_done, n0 + 2 * B + g)
                        act.activation(ht[g - 1], bank[g - 1], ACT.Copy).then_inc(ht_ready, 1)
                for g in range(G):
                    if g == G - 1:
                        norm_rows1(G, 0, rows(bank[0]), zn[0], zn_ready)
                    act.wait_ge(rms_ready, n0 + g + 1)
                    act.wait_ge(qkv1_done, n0 + g + 1)
                    s = 4 + 2 * (g % 2)
                    o = psum[:, s:s + 2, :].rearrange("p b n -> p (b n)")
                    for t in range(TILES):
                        k = g * TILES + t
                        last = act.activation(qkv1[g][:, t, :], o[:, t * QKV1:(t + 1) * QKV1], ACT.Copy, scale=rsmall[:, 0, k:k + 1])
                    last.then_inc(qkv1_ready, 1)

                def take_ffn(g):
                    act.wait_ge(ffn_done, n0 + g + 1)
                    act.activation(xn1[g].rearrange("p t d -> p (t d)"), bank[g], ACT.Copy).then_inc(ffn_ready, 1)

                for i in range(STEPS + 2):
                    if 1 <= i <= STEPS:
                        k, g = (i - 1) // G, (i - 1) % G
                        act.wait_ge(znt_done, n0 * BLOCKS + i)
                        act.activation(gt[g], bank[4 + g], ACT.Gelu, scale=ln_g[:, k:k + 1], bias=ln_b[:, k:k + 1]).then_inc(gt_ready, 1)
                    if 1 <= i < STEPS:
                        norm_rows1(G + i, i % G, rows(bank[i % G]), zn[i % G], zn_ready)
                    if i == STEPS + 1:
                        load_table(ACT.Exp)
                        split_qk(n0 + ROUNDS0, 1.0)
                    if i >= STEPS - G + 2:
                        take_ffn(i - (STEPS - G + 2))

                def take_rows1(g):
                    wait_alone(act, rows_done, n0 + g + 1)
                    store_rows(n0 + g, Q0)

                for r in range(2 * G):
                    exps(n0 * 2 + ROUNDS0 + r, (lambda: take_rows1((r - 3) // 2)) if r % 2 == 1 and r > 1 else None)
                    if r % 2 == 1 and r < 2 * G - 1:
                        split_qk(n0 + ROUNDS0 + (r + 1) // 2, 1.0)
                    if r % 2 == 0 and r:
                        copy_y(n0 * 2 + ROUNDS0 + r - 1, y1t[r // 2 - 1])
                copy_y(n0 * 2 + ROUNDS0 + 2 * G - 1, y1t[G - 1])
                load_table(ACT.Gelu)
                take_rows1(G - 1)

        GROUP_LINKS = (2 * LNS + 3) * G + 2

        @block.vector
        def _(dve):
            chain = Chain(dve, dve_chain, 0)
            dve.wait_ge(x_loaded0, X_LOADS)
            for t in range(TT):
                if t == TT // 2:
                    dve.wait_ge(x_loaded1, X_LOADS + 16)
                last = dve.bn_stats(stats[:, t, :], x_all[:, t // TILES, t % TILES, :])
            chain.step(last)
            for t in range(TT):
                last = dve.bn_aggr(mv[:, t, :], stats[:, t, :])
            chain.step(last)
            dve.tensor_scalar(var[:, :], mv[:, :, 1], EPS, None, ALU.add).then_inc(var_ready, 1)

            def norm_rows(b, dst):
                for t in range(TILES):
                    last = dve.tensor_scalar(dst[:, t, :], x_all[:, b, t, :], mv_b[:, b, t, 0:1], rstd_b[:, b, t:t + 1],
                                             ALU.subtract, ALU.mult)
                last.then_inc(row_ready, 1)

            def take_logits(b, s):
                dve.wait_ge(logits_done, b + 1)
                dve.tensor_copy(logits_b[:, b, :, :], bank[2 + s][:, 0:TILES * E].rearrange("p (t e) -> p t e", e=E)).then_inc(logits_taken, 1)

            def split_xt(b):
                dve.wait_ge(xt_hi_ready, b + 1)
                dve.tensor_tensor(xt_lo[:, :], Q0, xt_hi[:, :].bitcast(F32), ALU.subtract).then_inc(xt_lo_ready, 1)

            def split_qk(n, scale):
                dve.wait_ge(qk_hi_ready, n * 2 + 1)
                dve.scalar_tensor_tensor(qk_lo[:, 0, :], Q0, scale, qk_hi[:, 0, :].bitcast(F32),
                                         ALU.mult, ALU.subtract).then_inc(qk_lo_ready, 1)
                dve.wait_ge(qk_hi_ready, n * 2 + 2)
                dve.tensor_tensor(qk_lo[:, 1, :], Q1, qk_hi[:, 1, :].bitcast(F32), ALU.subtract).then_inc(qk_lo_ready, 1)

            def take_turned(rnd, c):
                dve.wait_ge(turned, rnd * NCH + c + 1)
                for h, t, o in CHUNKS[c]:
                    last = dve.tensor_copy(pt[:, h, 0:t + 1, t, :], turn_bank[c % 2][:, o:o + P * (t + 1)].rearrange("p (j q) -> p j q", q=P))
                last.then_inc(pt_ready, 1)

            def row_maxima(rnd, c):
                dve.wait_ge(scored, rnd * NCH + c + 1)
                for h, t, o in CHUNKS[c]:
                    last = dve.tensor_reduce(mneg[:, h, SLOT[t]:SLOT[t] + 1], score_bank[c % 3][:, o:o + P * (t + 1)], AX, ALU.max, negate=True)
                last.then_inc(max_ready, 1)

            def invert_sums(rnd, c):
                dve.wait_ge(exp_done, rnd * NCH + c + 1)
                h, s = CHUNKS[c][0][0], SLOT[CHUNKS[c][0][1]]
                s = slice(s, s + len(CHUNKS[c]))
                dve.reciprocal(rinv[:, h, s], rsum[:, h, s]).then_inc(rinv_ready, 1)

            for s in range(2):
                dve.wait_ge(rstd_ready, s + 1)
                norm_rows(s, xn_setup[s])
            dve.wait_ge(hi_setup, 1)
            dve.tensor_tensor(wqkv_lo[:, :, :, :].rearrange("p a b n -> p (a b n)"), wqkv_raw,
                              wqkv_hi[:, :, :, :].rearrange("p a b n -> p (a b n)").bitcast(F32), ALU.subtract).then_inc(lo_setup, 1)
            dve.wait_ge(rstd_ready, B)
            with dve.Fori(0, B // 2 - 1) as i:
                for s in range(2):
                    wait_alone(dve, tr_done, i * 2 + s + 1)
                    norm_rows(i * 2 + (s + 2), xn_setup[s])
                    take_logits(i * 2 + s, s)
            for s in range(2):
                take_logits(B - 2 + s, s)
            dve.wait_ge(logits_taken, B)
            norm_rows(0, xn)
            def over_experts(v):
                return v.unsqueeze(2).to_broadcast([P, TT, E])

            sm, ri = rsmall[:, 0, :], rsmall[:, 1, :]
            chain.step(dve.tensor_reduce(sm, logits, AX, ALU.max, negate=True))
            dve.tensor_tensor(rl, logits, over_experts(sm), ALU.add).then_inc(rl_ready, 1)
            split_xt(0)
            dve.wait_ge(rexp_done, 1)
            chain.step(dve.tensor_reduce(sm, rexp, AX, ALU.add))
            chain.step(dve.reciprocal(ri, sm))
            split_qk(0, SCALE0)
            chain.step(dve.tensor_tensor(rl, rexp, over_experts(ri), ALU.mult))
            dve.wait_ge(w_loaded, W_LOADS)
            chain.step(dve.tensor_tensor(corr[:, :, 0:E], rl, ebias[:, :].unsqueeze(1).to_broadcast([P, TT, E]), ALU.add))
            for t in range(TT):
                last = dve.max(top8[:, t, :], corr[:, t, 0:E])
            chain.step(last)
            for c in range(3):
                row_maxima(0, c)
            chain.step(dve.memset(top8[:, :, TOPK:8], GONE))
            dve.wait_ge(const_ready, 1)
            for t in range(TT):
                last = dve.match_replace(left[:, t, :], top8[:, t, :], corr[:, t, :], TAKEN)
            chain.step(last)
            for c in range(3):
                row_maxima(0, c + 3)
                invert_sums(0, c)
            chain.step(dve.tensor_tensor(comb, left[:, :, 0:E], corr[:, :, 0:E], ALU.not_equal))
            chain.step(dve.tensor_tensor(comb, comb, rl, ALU.mult))
            chain.step(dve.tensor_reduce(sm, comb, AX, ALU.add))
            chain.step(dve.tensor_scalar(sm, sm, NORM_MIN, None, ALU.max))
            chain.step(dve.reciprocal(ri, sm))
            chain.step(dve.tensor_tensor(comb, comb, over_experts(ri), ALU.mult))
            for c in range(3, NCH):
                invert_sums(0, c)
            split_qk(1, SCALE0)
            chain.step(dve.tensor_copy(comb3[:, :, 0:E], comb))
            chain.step(dve.tensor_tensor(comb, comb, comb3[:, :, 0:E], ALU.subtract))
            chain.step(dve.tensor_copy(comb3[:, :, E:2 * E], comb))
            dve.tensor_tensor(comb3[:, :, 2 * E:3 * E], comb, comb3[:, :, E:2 * E], ALU.subtract).then_inc(comb_ready, 1)
            LAG = 2

            def attend(turn, score):
                for c in range(NCH):
                    if turn is not None:
                        take_turned(turn, c)
                    if score is not None:
                        row_maxima(score, c)
                        if c >= LAG:
                            invert_sums(score, c - LAG)
                if score is not None:
                    for c in range(NCH - LAG, NCH):
                        invert_sums(score, c)

            def hidden(n, s, wait_buffer):
                dve.wait_ge(silu_done, n + 1)
                dve.tensor_tensor(sg[:, s, :], sg[:, s, :], UNIT_BANKS[s][1], ALU.mult).then_inc(su_done, 1)
                dve.wait_ge(su_done, n + 1)
                if wait_buffer is not None:
                    dve.wait_ge(down_done, wait_buffer)
                dve.tensor_tensor(hm[:, s, :], sg[:, s, :], UNIT_BANKS[s][2], ALU.mult).then_inc(hm_ready, 1)

            def first_pair(b):
                split_xt(b)
                split_qk(b * PAIRS, SCALE0)
                attend(None, b * PAIRS)
                split_qk(b * PAIRS + 1, SCALE0)

            def first_layer(b, last=False):
                with dve.Fori(0, PAIRS - 2) as p:
                    pair = b * PAIRS + p
                    attend(pair, pair + 1)
                    split_qk(pair + 2, SCALE0)
                pair = b * PAIRS + PAIRS - 1
                attend(pair - 1, pair)
                attend(pair, None)
                for u in range(3):
                    hidden(b * UNITS + u, u % 2, b * UNITS + 1 if u == 2 else None)
                if not last:
                    wait_alone(dve, tr_done, b + (B + 1))
                    norm_rows(b + 1, xn)
                with dve.Fori(0, (UNITS - 3) // 2) as i:
                    for s in range(2):
                        hidden(b * UNITS + i * 2 + (s + 3), (s + 1) % 2, b * UNITS + i * 2 + (s + 2))

            with dve.Fori(0, B - 1) as b:
                first_layer(b)
                first_pair(b + 1)
            first_layer(B - 1, last=True)

            setup_links = chain.n
            with dve.Fori(0, GROUPS) as q:
                n0 = q * G
                chain = Chain(dve, dve_chain, q * GROUP_LINKS + setup_links)

                def row_stats(n, g, src):
                    s = slice(g * TILES, (g + 1) * TILES)
                    for t in range(TILES):
                        last = dve.bn_stats(stats[:, g * TILES + t, :], src[:, t, :])
                    chain.step(last)
                    dve.sem_inc(waits_over, 1)
                    for t in range(TILES):
                        last = dve.bn_aggr(mv[:, g * TILES + t, :], stats[:, g * TILES + t, :])
                    chain.step(last)
                    dve.tensor_scalar(nmean[:, s], mv[:, s, 0], -1.0, None, ALU.mult)
                    dve.tensor_scalar(var[:, s], mv[:, s, 1], EPS, None, ALU.add).then_inc(var_ready, 1)

                def square_qk(g):
                    dve.wait_ge(qkv1_ready, n0 + g + 1)
                    chain.step(dve.tensor_tensor(sq1[g], qkv1[g][:, :, 0:QK], qkv1[g][:, :, 0:QK], ALU.mult))
                    chain.step(dve.tensor_reduce(ss1[:, g, :].rearrange("p (t h) -> p t h", t=TILES), sq1[g].rearrange("p t (h d) -> p t h d", d=HD1), AX, ALU.add))
                    dve.tensor_scalar(ss1[:, g, :], ss1[:, g, :], EPS_L2 * EPS_L2, None, ALU.max).then_inc(ss1_ready, 1)

                def norm_qk(g):
                    dve.wait_ge(rn1_ready, n0 + g + 1)
                    rn = rn1[:, g, :].rearrange("p (t h) -> p t h", t=TILES)
                    chain.step(dve.tensor_scalar(rn[:, :, 0:H1], rn[:, :, 0:H1], temp1[:, 1:2], None, ALU.mult))
                    qv = qkv1[g][:, :, 0:H1 * HD1].rearrange("p t (h d) -> p t h d", d=HD1)
                    kv = qkv1[g][:, :, H1 * HD1:QK].rearrange("p t (h d) -> p t h d", d=HD1)
                    dve.tensor_tensor(qv, qv, rn[:, :, 0:H1].unsqueeze(3).to_broadcast([P, TILES, H1, HD1]), ALU.mult)
                    kn_v = kn1[g].rearrange("p t (h r d) -> p t h r d", r=H1 // KV1, d=HD1)
                    for r in range(H1 // KV1):
                        last = dve.tensor_tensor(kn_v[:, :, :, r, :], kv,
                                                 rn[:, :, H1:H1 + KV1].unsqueeze(3).to_broadcast([P, TILES, KV1, HD1]), ALU.mult)
                    last.then_inc(qkn_ready, 1)

                def add_hidden(i):
                    k, g = i // G, i % G
                    dve.wait_ge(f_done, n0 * (BLOCKS - 1) + i + 1)
                    dve.scalar_tensor_tensor(ht[g], bank[g], bias_col[:, 2 * k + 1:2 * k + 2], ht[g], ALU.add, ALU.add).then_inc(h_ready, 1)

                dve.wait_ge(rows_ready, n0 + G)
                x1 = [x_all[:, n0 + g, :, :] for g in range(G)]
                for g in range(G):
                    row_stats(g, g, x1[g])
                dve.wait_ge(rows_ready, n0 + B)
                for g in range(1, G, 2):
                    dve.wait_ge(rstd_ready, q * LNS * G + (B + g + 1))
                    for t in range(TILES):
                        k = g * TILES + t
                        last = dve.tensor_scalar(xn1[g][:, t, :], x1[g][:, t, :], mv[:, k, 0:1], rstd[:, k:k + 1], ALU.subtract, ALU.mult)
                    last.then_inc(odd_row_ready, 1)
                s = slice(0, G * TILES)
                dve.wait_ge(rstd_ready, q * LNS * G + (B + G))
                chain.step(dve.tensor_tensor(rsmall[:, 1, s], rstd[:, s], rstd[:, s], ALU.mult))
                chain.step(dve.tensor_tensor(rsmall[:, 1, s], rsmall[:, 1, s], mv[:, s, 1], ALU.mult))
                dve.tensor_scalar(rsmall[:, 1, s], rsmall[:, 1, s], EPS_RMS, None, ALU.add).then_inc(ms_ready, 1)
                for i in range(STEPS):
                    if 3 <= i < STEPS - G + 3:
                        add_hidden(i - 3)
                    dve.wait_ge(lin_done, n0 * BLOCKS + i + 1)
                    row_stats(G + i, i % G, rows(bank[i % G]))
                    if i < G:
                        square_qk(i)
                    elif i < 2 * G:
                        dve.tensor_tensor(xn1[i - G], xn1[i - G], x1[i - G], ALU.add).then_inc(xr_ready, 1)
                    if i >= STEPS - G:
                        norm_qk(i - (STEPS - G))
                split_qk(n0 + ROUNDS0, 1.0)
                for r in range(2 * G + 1):
                    rnd = n0 * 2 + ROUNDS0 + r
                    attend(n0 * 2 + (ROUNDS0 + r - 1) if r else None, rnd if r < 2 * G else None)
                    if r % 2 == 1 and r < 2 * G - 1:
                        split_qk(n0 + ROUNDS0 + (r + 1) // 2, 1.0)
                assert chain.n == GROUP_LINKS, chain.n

        @block.tensor
        def _(pe):
            mm = nc.tensor.matmul
            K = dict(skip_group_check=True)

            def transpose_rows(dst, src):
                for t in range(TILES):
                    last = nc.tensor.transpose(dst[:, t * P:(t + 1) * P], src[:, t, :], ident[:, :])
                return last

            pe.wait_ge(const_ready, 1)

            def turn_rows(b, s):
                pe.wait_ge(row_ready, b + 1)
                transpose_rows(bank[s], xn_setup[s]).then_inc(tr_done, 1)

            def router_logits(b, s):
                pe.wait_ge(xt_copied, b + 1)
                for t in range(TILES):
                    last = mm(bank[2 + s][:, t * E:(t + 1) * E], xt_setup[s][:, t * P:(t + 1) * P], rw_raw[:, :], start=True, stop=True)
                last.then_inc(logits_done, 1)

            turn_rows(0, 0)
            turn_rows(1, 1)
            with pe.Fori(0, B // 2 - 1) as i:
                for s in range(2):
                    router_logits(i * 2 + s, s)
                    turn_rows(i * 2 + (s + 2), s)
            router_logits(B - 2, 0)
            pe.wait_ge(logits_taken, B - 2)
            router_logits(B - 1, 1)
            pe.wait_ge(w_loaded, W_LOADS)
            for i in range(NLIN):
                o = psum[:, 6:8, :].rearrange("p b n -> p (b n)")[:, i * D:(i + 1) * D]
                last = mm(o, la[:, i, :], lb[:, i, :], start=True, stop=True)
            last.then_inc(lora_done, 1)
            pe.wait_ge(lora_taken, 2)

            def project_qk(n):
                pe.wait_ge(wst_ready, n * 2 + 2)
                for i, rb in enumerate((Q0, Q1)):
                    split_matmul(nc, rb, (wst_hi[:, i, :], wst_lo[:, i, :]), (xt_hi[:, :], xt_lo[:, :]), True, True).then_inc(qk_done, 1)

            def project_values(b):
                for f in range(FILLS):
                    t, half = f // VHALVES, f % VHALVES
                    if f >= 2:
                        pe.wait_ge(v_taken, b * FILLS + f - 1)
                    c, n = slice(t * P, (t + 1) * P), PAIRS // VHALVES
                    w = [v[:, 2, half * n:(half + 1) * n, :].rearrange("p n m -> p (n m)") for v in (wqkv_hi, wqkv_lo)]
                    split_matmul(nc, bank[3 + f % 2], (xt_hi[:, c], xt_lo[:, c]), w, True, True).then_inc(v_done, 1)

            def score_chunk(rnd, c, head_rows, first_round):
                if c >= 3 or not first_round:
                    pe.wait_ge(exp_done, rnd * NCH + (c - 2))
                sc = score_bank[c % 3]
                for i, (h, t, o) in enumerate(CHUNKS[c]):
                    r = head_rows[h]
                    w = P * (t + 1)
                    qs_, ks = slice(t * P, (t + 1) * P), slice(0, w)
                    split_matmul(nc, sc[:, o:o + w], (qk_hi[r, 0, qs_], qk_lo[r, 0, qs_]), (qk_hi[r, 1, ks], qk_lo[r, 1, ks]), i == 0, False, **K)
                    last = mm(sc[:, o + w - P:o + w], identb[:, :], causal[:, :], start=False, stop=True, **K)
                last.then_inc(scored, 1)

            def turn_chunk(rnd, c):
                pe.wait_ge(normed, rnd * NCH + c + 1)
                if c >= 2:
                    pe.wait_ge(pt_ready, rnd * NCH + (c - 1))
                for h, t, o in CHUNKS[c]:
                    for j in range(t + 1):
                        s = h * HALF + PROB[t] + j * P
                        last = nc.tensor.transpose(turn_bank[c % 2][:, o + j * P:o + (j + 1) * P], probs[:, s:s + P], ident[:, :])
                last.then_inc(turned, 1)

            def attend(turn, score, head_rows, qk, first_round=False, middle=None, ahead=None):
                for c in range(NCH):
                    if turn is not None and not (c == 0 and ahead is not None):
                        turn_chunk(turn, c)
                    if score is not None:
                        if c == 0:
                            pe.wait_ge(qk_lo_ready, qk * 2 + 2)
                        score_chunk(score, c, head_rows, first_round)
                    if c == 0 and ahead is not None:
                        ahead()
                        turn_chunk(turn, c)
                    if c == 2 and middle is not None:
                        middle()

            def weigh_values(rnd, v, m, col0):
                pe.wait_ge(pt_ready, rnd * NCH + NCH)
                for k in range(TILES):
                    for h in range(2):
                        c = col0 + h * m
                        last = mm(Y[c:c + m, k * P:T], v(k, h), pt[:, h, k, k:TILES, :].rearrange("p t q -> p (t q)"),
                                  start=(k == 0), stop=(k == TILES - 1), tile_position=(0, c), **K)
                last.then_inc(y_done, 1)

            ROWS0 = [slice(0, DQ), slice(DQ, 2 * DQ)]

            def weigh_pair(n):
                pe.wait_ge(v_ready, n + 1)
                weigh_values(n, lambda k, h: v0[:, k, h * DQ:(h + 1) * DQ], DQ, 0)

            def project_unit(u, n, s, wait_bank):
                pe.wait_ge(gst_ready, 2 * n + 2)
                if wait_bank:
                    pe.wait_ge(hm_ready, n - 1)
                for i in range(2):
                    split_matmul(nc, UNIT_BANKS[s][i], (gst_hi[:, s, i * P:(i + 1) * P], gst_lo[:, s, i * P:(i + 1) * P]),
                                 (xt_hi[:, :], xt_lo[:, :]), True, True)
                mm(UNIT_BANKS[s][2], csel[:, u, :], combt[:, :], start=True, stop=True).then_inc(gu_done, 1)

            def unit_down(u, n, s):
                pe.wait_ge(hm_ready, n + 1)
                for t in range(TILES):
                    last = mm(ACC[:, t * P:(t + 1) * P], hm[:, s, t * P:(t + 1) * P], down[:, u, :], start=False, stop=False, **K)
                return last.then_inc(down_done, 1)

            def project_out(t):
                for p in range(PAIRS):
                    last = mm(ACC[:, t * P:(t + 1) * P], yt[:, p, t * P:(t + 1) * P], w_out0[:, p, :], start=False, stop=False, **K)
                return last

            def first_rows(b):
                pe.wait_ge(row_ready, b + (B + 1))
                transpose_rows(Q0, xn).then_inc(tr_done, 1)

            def turn_weights(b):
                pe.wait_ge(comb_ready, 1)
                for t in range(TILES):
                    last = nc.tensor.transpose(Q0.bitcast(BF16)[:, t * P:(t + 1) * P], comb3_b[:, b, t, :], identb[:, :])
                last.then_inc(combt_done, 1)

            def first_projections(b):
                pe.wait_ge(xt_lo_ready, b + 1)
                project_qk(b * PAIRS)
                project_values(b)

            def first_scores(b, chunks):
                for c in chunks:
                    if c == 0:
                        pe.wait_ge(qk_lo_ready, b * PAIRS * 2 + 2)
                    score_chunk(b * PAIRS, c, ROWS0, True)

            def first_layer(b):
                with pe.Fori(0, PAIRS - 2) as p:
                    pair = b * PAIRS + p
                    attend(pair, pair + 1, ROWS0, pair + 1)
                    project_qk(pair + 2)
                    weigh_pair(pair)
                pair = b * PAIRS + PAIRS - 1
                attend(pair - 1, pair, ROWS0, pair)
                weigh_pair(pair - 1)
                turn_weights(b)
                for c in range(3):
                    turn_chunk(pair, c)
                wait_alone(pe, exp_done, pair * NCH + NCH)
                wait_alone(pe, combt_ready, b + 1)
                project_unit(0, b * UNITS, 0, False)
                for c in range(3, NCH):
                    turn_chunk(pair, c)
                weigh_pair(pair)
                project_unit(1, b * UNITS + 1, 1, False)
                pe.wait_ge(y_ready, pair + 1)
                mm(ACC, ident[:, :], x_all[:, b, :, :].rearrange("p t d -> p (t d)"), start=True, stop=False, **K)
                project_unit(2, b * UNITS + 2, 0, True)
                unit_down(0, b * UNITS, 0)
                with pe.Fori(0, (UNITS - 3) // 2) as i:
                    for s in range(2):
                        n = b * UNITS + i * 2 + (s + 3)
                        project_unit(i * 2 + (s + 3), n, (s + 1) % 2, True)
                        unit_down(i * 2 + (s + 1), n - 2, (s + 1) % 2)

            def last_unit(b, u):
                unit_down(u, b * UNITS + u, u % 2)

            pe.wait_ge(lo_setup, 1)
            first_rows(0)
            first_projections(0)
            first_scores(0, range(NCH))
            project_qk(1)
            pe.wait_ge(v_taken, FILLS)
            pe.wait_ge(act_setup, 4)
            with pe.Fori(0, B - 1) as b:
                first_layer(b)
                first_rows(b + 1)
                last_unit(b, UNITS - 2)
                project_out(0)
                last_unit(b, UNITS - 1)
                first_projections(b + 1)
                first_scores(b + 1, range(3))
                project_out(1)
                first_scores(b + 1, range(3, NCH))
                project_qk((b + 1) * PAIRS + 1)
                project_out(2)
                project_out(3).then_inc(acc_done, 1)
            first_layer(B - 1)
            last_unit(B - 1, UNITS - 2)
            last_unit(B - 1, UNITS - 1)
            for t in range(TILES):
                last = project_out(t)
            last.then_inc(acc_done, 1)

            pe.wait_ge(lin_ready, 1)
            with pe.Fori(0, GROUPS) as q:
                n0 = q * G
                def turn_qk(g):
                    pe.wait_ge(qkn_ready, n0 + g + 1)
                    transpose_rows(Q0, qkv1[g][:, :, 0:H1 * HD1]).then_inc(qk_done, 1)
                    transpose_rows(Q1, kn1[g]).then_inc(qk_done, 1)

                def weigh_round(r):
                    g, j = r // 2, r % 2
                    v1 = (H1 + KV1 + j) * HD1
                    weigh_values(n0 * 2 + ROUNDS0 + r, lambda k, h: qkv1[g][:, k, v1:v1 + HD1], HD1, 2 * j * HD1)

                def ffn_in(i):
                    k, g = i // G, i % G
                    if k:
                        pe.wait_ge(h_ready, n0 * (BLOCKS - 1) + i - G + 1)
                    mm(bank[g], bias_on[0:96, :], bias_bf[0:96, 2 * k, :].unsqueeze(1).to_broadcast([96, TILES, D]), start=True, stop=False, **K)
                    for t in range(TILES):
                        last = mm(bank[g][:, t * P:(t + 1) * P], ht[g][:, t * P:(t + 1) * P], lin[:, 2 * k, :], start=False, stop=True, **K)
                    last.then_inc(lin_done, 1)

                def ffn_out(i):
                    k, g = i // G, i % G
                    pe.wait_ge(gt_ready, n0 * BLOCKS + i + 1)
                    if k < BLOCKS - 1:
                        mm(bank[g], lin[:, 2 * k + 1, :], gt[g], start=True, stop=True).then_inc(f_done, 1)
                        return
                    mm(bank[g], bias_on[0:96, :], bias_bf[0:96, NLIN - 1, :].unsqueeze(1).to_broadcast([96, TILES, D]), start=True, stop=False, **K)
                    pe.wait_ge(xr_ready, n0 + g + 1)
                    mm(bank[g], ident[:, :], xn1[g].rearrange("p t d -> p (t d)"), start=False, stop=False, **K)
                    for t in range(TILES):
                        c = slice(t * P, (t + 1) * P)
                        mm(bank[g][:, c], ht[g][:, c], ident[:, :], start=False, stop=False, **K)
                        last = mm(bank[g][:, c], gt[g][:, c], lin[:, NLIN - 1, :], start=False, stop=True, **K)
                    last.then_inc(ffn_done, 1)

                for g in range(G):
                    if g % 2 == 0:
                        pe.wait_ge(row_ready, q * (G // 2) + (2 * B + g // 2 + 1))
                    else:
                        pe.wait_ge(odd_row_ready, q * (G // 2) + (g // 2 + 1))
                    transpose_rows(bank[g], xn1[g]).then_inc(tr_done, 1)
                for g in range(G):
                    pe.wait_ge(ht_ready, n0 + g + 1)
                    if g >= 2:
                        pe.wait_ge(qkv1_ready, n0 + g - 1)
                    s = 4 + 2 * (g % 2)
                    o = psum[:, s:s + 2, :].rearrange("p b n -> p (b n)")
                    for t in range(TILES):
                        last = mm(o[:, t * QKV1:(t + 1) * QKV1], ht[g][:, t * P:(t + 1) * P], wqkv1[:, :], start=True, stop=True)
                    last.then_inc(qkv1_done, 1)
                    ffn_in(g)
                for i in range(1, STEPS + 2):
                    if G <= i + 1 < STEPS:
                        ffn_in(i + 1)
                    if i == STEPS + 1:
                        turn_qk(0)
                    if i >= 2:
                        ffn_out(i - 2)
                    if i <= STEPS:
                        if i in (1, 3):
                            pe.wait_ge(qkv1_ready, n0 + G - 1 + i // 2)
                        pe.wait_ge(zn_ready, n0 * BLOCKS + i)
                        transpose_rows(bank[4 + (i - 1) % G], zn[(i - 1) % G]).then_inc(znt_done, 1)

                def output_rows(g):
                    pe.wait_ge(y_ready, n0 + (ROUNDS0 + g + 1))
                    mm(Q0, ident[:, :], xn1[g].rearrange("p t d -> p (t d)"), start=True, stop=False, **K)
                    for t in range(TILES):
                        c = slice(t * P, (t + 1) * P)
                        last = mm(Q0[:, c], y1t[g][:, c], wo1[:, :], start=False, stop=True, **K)
                    last.then_inc(rows_done, 1)

                pe.wait_ge(ffn_ready, n0 + G)
                for r in range(2 * G):
                    odd = r % 2 == 1
                    head_rows = [slice((2 * (r % 2) + h) * HD1, (2 * (r % 2) + h + 1) * HD1) for h in range(2)]
                    attend(n0 * 2 + (ROUNDS0 + r - 1) if r else None, n0 * 2 + ROUNDS0 + r, head_rows, n0 + (ROUNDS0 + r // 2),
                           first_round=(r == 0), middle=(lambda: output_rows((r - 3) // 2)) if odd and r > 1 else None,
                           ahead=(lambda: weigh_round(r - 2)) if odd and r > 1 else None)
                    if odd and r < 2 * G - 1:
                        if r > 1:
                            pe.wait_ge(rows_ready, n0 + (B + (r - 1) // 2))
                        turn_qk((r + 1) // 2)
                    if odd:
                        weigh_round(r - 1)
                attend(n0 * 2 + (ROUNDS0 + 2 * G - 1), None, None, None)
                weigh_round(2 * G - 1)
                output_rows(G - 1)


def kernel(**inputs):
    import numpy as _np
    import concourse.bacc as _bacc
    from concourse import mybir as _mybir
    from concourse.bass_utils import run_bass_kernel_spmd as _run

    g = {k: _np.asarray(v) for k, v in inputs.items()}

    def heads_first(w):
        return w.transpose(1, 2, 0).reshape(D, H0 * DQ)

    gu = g["L0_ffn_gate_up_proj"].reshape(E // 2, 2, 2, I, D)
    gu = gu.transpose(4, 0, 2, 1, 3).reshape(D, E // 2, 2 * P)
    shared = _np.concatenate([g["L0_ffn_shared_gate_w"], g["L0_ffn_shared_up_w"]], 0).T.reshape(D, 1, 2 * P)
    dn = g["L0_ffn_down_proj"].transpose(0, 2, 1).reshape(E // 2, P, D).transpose(1, 0, 2)
    shared_dn = g["L0_ffn_shared_down_w"].T.reshape(P, 1, D)
    lay = {
        "x": g["L0_attn_x"],
        "wqkv": _np.concatenate([heads_first(g[f"L0_attn_{n}"]) for n in "QKV"], 1),
        "w_out0": g["L0_attn_W"].transpose(2, 1, 0).reshape(PAIRS, P, D).transpose(1, 0, 2),
        "router": g["L0_ffn_router_weight"].T,
        "ebias": g["L0_ffn_e_score_bias"],
        "gu": _np.concatenate([shared, gu], 1),
        "down": _np.concatenate([shared_dn, dn], 1),
        "wqkv1": _np.concatenate([g["L1_attn_Wq"], g["L1_attn_Wk"], g["L1_attn_Wv"]], 1),
        "norm_w": g["L1_attn_norm_w"].reshape(D, 1),
        "wo1": g["L1_attn_Wo"],
        "gate1": g["L1_attn_gate"].reshape(1),
        "temp1": g["L1_attn_log_temperature"].reshape(1),
        "qw": g["L1_ffn_qweights"].transpose(2, 0, 1),
        "qs": g["L1_ffn_scales"].transpose(2, 0, 1),
        "la": g["L1_ffn_lora_a"].transpose(1, 0, 2),
        "lb": g["L1_ffn_lora_b"].transpose(2, 0, 1),
        "bias_col": g["L1_ffn_biases"].T,
        "bias_row": g["L1_ffn_biases"],
        "ln_g": g["L1_ffn_ln_gamma"].T,
        "ln_b": g["L1_ffn_ln_beta"].T,
    }
    nc = _bacc.Bacc("TRN2", target_bir_lowering=False, num_devices=1)
    arrays, args = {}, {}
    for name, v in lay.items():
        v = _np.ascontiguousarray(v)
        arrays[f"in_{name}"] = v
        args[name] = nc.dram_tensor(f"in_{name}", v.shape, _mybir.dt.from_np(v.dtype), kind="ExternalInput").ap()
    out = nc.dram_tensor("out_rows", (B, T, D), F32, kind="ExternalOutput").ap()
    build(nc, args, out)
    r = _run(nc, [arrays], core_ids=[0])
    return r.results[0]["out_rows"]
```
